# Optimizing a Trainium2 kernel written in Bass

```python
import numpy as np
import jax
import jax.numpy as jnp

def _softmax(x, axis=-1):
    return jax.nn.softmax(x, axis=axis)

def _gelu(x):
    return jax.nn.gelu(x, approximate=True)

def _silu(x):
    return jax.nn.silu(x)

def _sigmoid(x):
    return jax.nn.sigmoid(x)

def _layernorm(x, axis=-1, eps=1e-05):
    m = jnp.mean(x, axis=axis, keepdims=True)
    v = jnp.var(x, axis=axis, keepdims=True)
    return (x - m) / jnp.sqrt(v + eps)

def _scatter_add(tgt, idx, src, axis=0):
    return tgt.at[idx].add(src)

def _segment_sum(src, seg, n):
    return jax.ops.segment_sum(src, seg, n)
kernel_name = 'mk_rec_standalone_d1_rec_r8_e3ab16'

def setup_inputs(seed: int=0):
    np.random.seed(seed)
    _w = jnp.asarray

    def _rec_inputs():
        import jax
        import jax.numpy as jnp
        _rk = jax.random.key(seed)
        r_dense_features = -0.00338568 + 1.0005 * jax.random.normal(jax.random.fold_in(_rk, 1), (2048, 13), jnp.float32)
        r_sparse_features = jnp.stack([jax.random.randint(jax.random.fold_in(jax.random.fold_in(_rk, 2), 0), (2048,), 2, 12500, jnp.int32), jax.random.randint(jax.random.fold_in(jax.random.fold_in(_rk, 2), 1), (2048,), 1, 99999, jnp.int32), jax.random.randint(jax.random.fold_in(jax.random.fold_in(_rk, 2), 2), (2048,), 0, 12500, jnp.int32), jax.random.randint(jax.random.fold_in(jax.random.fold_in(_rk, 2), 3), (2048,), 5, 12500, jnp.int32), jax.random.randint(jax.random.fold_in(jax.random.fold_in(_rk, 2), 4), (2048,), 20, 99993, jnp.int32), jax.random.randint(jax.random.fold_in(jax.random.fold_in(_rk, 2), 5), (2048,), 0, 99993, jnp.int32), jax.random.randint(jax.random.fold_in(jax.random.fold_in(_rk, 2), 6), (2048,), 2, 99999, jnp.int32), jax.random.randint(jax.random.fold_in(jax.random.fold_in(_rk, 2), 7), (2048,), 2, 99995, jnp.int32), jax.random.randint(jax.random.fold_in(jax.random.fold_in(_rk, 2), 8), (2048,), 0, 99999, jnp.int32), jax.random.randint(jax.random.fold_in(jax.random.fold_in(_rk, 2), 9), (2048,), 2, 99986, jnp.int32), jax.random.randint(jax.random.fold_in(jax.random.fold_in(_rk, 2), 10), (2048,), 4, 99999, jnp.int32), jax.random.randint(jax.random.fold_in(jax.random.fold_in(_rk, 2), 11), (2048,), 15, 99999, jnp.int32), jax.random.randint(jax.random.fold_in(jax.random.fold_in(_rk, 2), 12), (2048,), 0, 99989, jnp.int32), jax.random.randint(jax.random.fold_in(jax.random.fold_in(_rk, 2), 13), (2048,), 5, 99990, jnp.int32), jax.random.randint(jax.random.fold_in(jax.random.fold_in(_rk, 2), 14), (2048,), 2, 99996, jnp.int32), jax.random.randint(jax.random.fold_in(jax.random.fold_in(_rk, 2), 15), (2048,), 3, 99994, jnp.int32), jax.random.randint(jax.random.fold_in(jax.random.fold_in(_rk, 2), 16), (2048,), 0, 99998, jnp.int32), jax.random.randint(jax.random.fold_in(jax.random.fold_in(_rk, 2), 17), (2048,), 13, 99998, jnp.int32), jax.random.randint(jax.random.fold_in(jax.random.fold_in(_rk, 2), 18), (2048,), 10, 12498, jnp.int32), jax.random.randint(jax.random.fold_in(jax.random.fold_in(_rk, 2), 19), (2048,), 0, 99999, jnp.int32), jax.random.randint(jax.random.fold_in(jax.random.fold_in(_rk, 2), 20), (2048,), 0, 99995, jnp.int32), jax.random.randint(jax.random.fold_in(jax.random.fold_in(_rk, 2), 21), (2048,), 1, 99998, jnp.int32), jax.random.randint(jax.random.fold_in(jax.random.fold_in(_rk, 2), 22), (2048,), 1, 99997, jnp.int32), jax.random.randint(jax.random.fold_in(jax.random.fold_in(_rk, 2), 23), (2048,), 2, 99989, jnp.int32), jax.random.randint(jax.random.fold_in(jax.random.fold_in(_rk, 2), 24), (2048,), 6, 12500, jnp.int32), jax.random.randint(jax.random.fold_in(jax.random.fold_in(_rk, 2), 25), (2048,), 2, 99995, jnp.int32)], axis=1)
        return (r_dense_features, r_sparse_features)
    r_dense_features, r_sparse_features = _rec_inputs()

    def _L0_rec_setup():
        import jax, jax.numpy as jnp
        import numpy as np
        NUM_TABLES = 26
        VOCAB = 12500
        EMBED_DIM = 64
        N_DENSE = 13
        LN_BOT = 64
        LN_TOP = 256
        BATCH = 2048
        key = jax.random.key(seed)
        ks = jax.random.split(key, 7)
        dense_features = jax.random.normal(ks[0], (BATCH, N_DENSE), dtype=jnp.float32)
        sparse_features = jax.random.randint(ks[1], (BATCH, NUM_TABLES), 0, VOCAB, dtype=jnp.int32)
        tables = jax.random.normal(ks[2], (NUM_TABLES, VOCAB, EMBED_DIM), dtype=jnp.float32) * 0.01
        W_bot = jax.random.normal(ks[3], (N_DENSE, LN_BOT), dtype=jnp.float32) * 0.1
        b_bot = jnp.zeros((LN_BOT,), dtype=jnp.float32)
        top_in = NUM_TABLES * EMBED_DIM + LN_BOT
        W_top = jax.random.normal(ks[4], (top_in, LN_TOP), dtype=jnp.float32) * 0.02
        b_top = jnp.zeros((LN_TOP,), dtype=jnp.float32)
        return {'dense_features': dense_features, 'sparse_features': sparse_features, 'tables': tables, 'W_bot': W_bot, 'b_bot': b_bot, 'W_top': W_top, 'b_top': b_top}
    _L0_rec_all = _L0_rec_setup()
    _L0_rec_in = {k: v for k, v in _L0_rec_all.items() if k in ('tables', 'W_bot', 'b_bot', 'W_top', 'b_top')}
    del _L0_rec_all
    return {'r_dense_features': r_dense_features, 'r_sparse_features': r_sparse_features, 'L0_rec_tables': _L0_rec_in['tables'], 'L0_rec_W_bot': _L0_rec_in['W_bot'], 'L0_rec_b_bot': _L0_rec_in['b_bot'], 'L0_rec_W_top': _L0_rec_in['W_top'], 'L0_rec_b_top': _L0_rec_in['b_top']}

def reference(r_dense_features, r_sparse_features, L0_rec_tables, L0_rec_W_bot, L0_rec_b_bot, L0_rec_W_top, L0_rec_b_top):
    import jax
    import jax.numpy as jnp

    def _L0_rec_ref(dense_features, sparse_features, tables, W_bot, b_bot, W_top, b_top):
        import jax, jax.numpy as jnp
        import numpy as np
        NUM_TABLES = 26
        VOCAB = 12500
        EMBED_DIM = 64
        N_DENSE = 13
        LN_BOT = 64
        LN_TOP = 256
        BATCH = 2048
        B = dense_features.shape[0]
        emb = jax.vmap(lambda tab, idx: tab[idx], in_axes=(0, 1))(tables, sparse_features)
        sparse_vec = jnp.transpose(emb, (1, 0, 2)).reshape(B, NUM_TABLES * EMBED_DIM)
        dense_vec = dense_features @ W_bot + b_bot
        z = jnp.concatenate([sparse_vec, dense_vec], axis=1)
        top = z @ W_top + b_top
        out = jax.nn.sigmoid(jnp.mean(top, axis=1))
        return out
    y = _L0_rec_ref(r_dense_features, r_sparse_features, L0_rec_tables, L0_rec_W_bot, L0_rec_b_bot, L0_rec_W_top, L0_rec_b_top)
    return y

_drawn_inputs = setup_inputs


def setup_inputs(seed=0):
    import zlib

    import numpy as np

    out = dict(_drawn_inputs(seed))
    spreads = {'L0_rec_b_bot': (0.0, 2.0), 'L0_rec_b_top': (0.0, 2.0)}
    factors = {'r_dense_features': 8.0, 'L0_rec_tables': 58.214, 'L0_rec_W_bot': 8.0, 'L0_rec_W_top': 8.0}
    for name, (base, spread) in spreads.items():
        noise = np.random.default_rng([zlib.crc32(name.encode()), seed]).standard_normal(out[name].shape)
        drawn = base * np.exp(spread * noise) if base else spread * noise
        out[name] = jnp.asarray(drawn.astype(out[name].dtype))
    for name, factor in factors.items():
        out[name] = (out[name] * factor).astype(out[name].dtype)
    return out
```

```python
from contextlib import ExitStack

import concourse.bass as bass
from concourse import mybir

P = 128
F32 = mybir.dt.float32
I32 = mybir.dt.int32
U32 = mybir.dt.uint32
ALU = mybir.AluOpType
ACT = mybir.ActivationFunctionType
AX = mybir.AxisListType

SLOTS = 8
RING = 4
ROW_BITS = 14
J_BITS = 5


def recommender_head(nc, dense, sparse, tables, w_bot_t, b_bot, w_top, b_top, out):
    T, VOCAB, D = tables.shape
    B, NF = dense.shape
    NTOP = w_top.shape[1]
    J = B // P
    L = J * T
    MAX_ROUNDS = L // SLOTS
    LAST = VOCAB - 1
    PAIRS = SLOTS // 2
    TP = T // 2
    DC = NF + 1
    assert B % P == 0 and D == 64 and T % 2 == 0 and L % SLOTS == 0
    assert VOCAB < 1 << ROW_BITS and J < 1 << J_BITS
    assert T << (ROW_BITS + J_BITS) <= 1 << 24
    assert MAX_ROUNDS % RING == 0

    table_rows = tables.rearrange("t v d -> (t v) d")

    with ExitStack() as ctx:
        def sb(name, shape, dt=F32):
            return ctx.enter_context(nc.sbuf_tensor(name, shape, dt))

        def psum(name, shape):
            return ctx.enter_context(nc.psum_tensor(name, shape, F32))

        def sem(name):
            return ctx.enter_context(nc.semaphore(name))

        idx = sb("idx", [P, L], I32)
        dense_sb = sb("dense_sb", [P, J, NF])
        wt_sb = sb("wt_sb", [P, TP, NTOP])
        wd_sb = sb("wd_sb", [D, NTOP])
        last_rows = sb("last_rows", [T, D])
        wbot_sb = sb("wbot_sb", [D, DC])
        btop_sb = sb("btop_sb", [D, NTOP // D])
        iota_t16k = sb("iota_t16k", [P, J, T])
        iota_j1 = sb("iota_j1", [P, J, T])
        iota_t = sb("iota_t", [P, SLOTS, T])
        iota_j = sb("iota_j", [P, J, SLOTS])
        iota_row = sb("iota_row", [P, P])
        iota_col = sb("iota_col", [P, 1])
        ident = sb("ident", [P, P])
        shift = sb("shift", [P, 2, 2, D])
        ones = sb("ones", [D, P])
        key_base = sb("key_base", [P, L])
        wrap = sb("wrap", [P, L])
        row = sb("row", [P, L])
        key_all = sb("key_all", [P, L])
        keys = sb("keys", [P, L])
        at_last = sb("at_last", [P, L])
        n_last = sb("n_last", [P, 1])
        n_min = sb("n_min", [1, 1])
        n_int = sb("n_int", [1, 1], I32)
        n_rounds = sb("n_rounds", [1, 1], I32)
        top = sb("top", [P, RING, SLOTS])
        code = sb("code", [P, RING, SLOTS], I32)
        tab_row = sb("tab_row", [P, RING, SLOTS], I32)
        tab = sb("tab", [P, RING, SLOTS], I32)
        jj = sb("jj", [P, RING, SLOTS], I32)
        flat = sb("flat", [P, RING, SLOTS], U32)
        got = sb("got", [P, RING, SLOTS, D])
        got_t = sb("got_t", [P, 2, PAIRS, P])
        is_tab = sb("is_tab", [P, SLOTS, T])
        picked = sb("picked", [P, SLOTS, T])
        dots = sb("dots", [P, SLOTS])
        is_j = sb("is_j", [P, J, SLOTS])
        by_j = sb("by_j", [P, J, SLOTS])
        round_sum = sb("round_sum", [P, J])
        acc = sb("acc", [P, J])
        wsum = sb("wsum", [P, TP])
        wdsum = sb("wdsum", [D, 1])
        w_blk = sb("w_blk", [P, 2, T])
        w_dense = sb("w_dense", [D, 1])
        bsum = sb("bsum", [D, 1])
        prods = sb("prods", [D, T + DC])
        coef = sb("coef", [P, T + DC])
        last_part = sb("last_part", [P, J, T])
        dense_part = sb("dense_part", [P, J, NF])
        last_sum = sb("last_sum", [P, J])
        dense_sum = sb("dense_sum", [P, J])
        warm = sb("warm", [1, 1])
        prob = sb("prob", [P, J])

        ps_turn = psum("ps_turn", [P, 2, PAIRS, P])
        ps_dots = psum("ps_dots", [P, 2, 512])
        ps_misc = psum("ps_misc", [P, 4, 512])

        idx_in = sem("idx_in")
        weights_in = sem("weights_in")
        small_in = sem("small_in")
        iotas_ready = sem("iotas_ready")
        vec = sem("vec")
        consts_ready = sem("consts_ready")
        keys_ready = sem("keys_ready")
        count_turned = sem("count_turned")
        count_ready = sem("count_ready")
        wsum_ready = sem("wsum_ready")
        w_moved = sem("w_moved")
        w_ready = sem("w_ready")
        rows_turned = sem("rows_turned")
        prods_ready = sem("prods_ready")
        coef_ready = sem("coef_ready")
        flat_ready = sem("flat_ready")
        gathered = [sem(f"gathered{b}") for b in range(RING)]
        turned = sem("turned")
        copied = sem("copied")
        scored = sem("scored")
        used = sem("used")
        acc_ready = sem("acc_ready")
        prob_ready = sem("prob_ready")
        stored = sem("stored")

        block = ctx.enter_context(nc.Block())

        @block.sync
        def _(sp):
            sp.dma_start(idx[:, :], sparse.rearrange("(p j) t -> p (j t)", p=P)).then_inc(idx_in, 16)
            sp.dma_start(wt_sb[:, :, :], w_top[0:T * D, :].rearrange("(c q) n -> q c n", q=P)).then_inc(weights_in, 16)
            sp.dma_start(wd_sb[:, :], w_top[T * D:T * D + D, :]).then_inc(weights_in, 16)
            sp.wait_ge(prob_ready, 1)
            sp.dma_start(out.rearrange("(p j) -> p j", p=P), prob[:, :]).then_inc(stored, 16)
            sp.wait_ge(stored, 16)

        @block.gpsimd
        def _(pool):
            pool.iota(iota_t16k[:, :, :], [[0, J], [1, T]], base=0,
                      channel_multiplier=0, allow_small_or_imprecise_dtypes=True).then_inc(iotas_ready, 1)
            pool.iota(iota_j1[:, :, :], [[1, J], [0, T]], base=1, channel_multiplier=0,
                      allow_small_or_imprecise_dtypes=True).then_inc(iotas_ready, 1)
            pool.iota(iota_t[:, :, :], [[0, SLOTS], [1, T]], base=0, channel_multiplier=0,
                      allow_small_or_imprecise_dtypes=True).then_inc(iotas_ready, 1)
            pool.iota(iota_j[:, :, :], [[1, J], [0, SLOTS]], base=1, channel_multiplier=0,
                      allow_small_or_imprecise_dtypes=True).then_inc(iotas_ready, 1)
            pool.iota(iota_row[:, :], [[1, P]], base=0, channel_multiplier=0,
                      allow_small_or_imprecise_dtypes=True).then_inc(iotas_ready, 1)
            pool.iota(iota_col[:, :], [[0, 1]], base=0, channel_multiplier=1,
                      allow_small_or_imprecise_dtypes=True).then_inc(iotas_ready, 1)

            due = pool.alloc_register("due")
            pool.reg_mov(due, 1)

            def gather(b):
                pool.wait_ge(flat_ready, due)
                pool.reg_add(due, due, 1)
                for s in range(SLOTS):
                    pool.indirect_dma_start(
                        got[:, b, s, :], None, table_rows,
                        bass.IndirectOffsetOnAxis(ap=flat[:, b, s:s + 1], axis=0),
                    ).then_inc(gathered[b], 16)

            gather(0)
            pool.wait_ge(count_ready, 1)
            n = pool.value_load(n_rounds[0:1, 0:1], min_val=0, max_val=MAX_ROUNDS)
            with pool.Fori(0, MAX_ROUNDS // RING) as i:
                for h in range(1, RING + 1):
                    with pool.If(i * RING + h < n):
                        gather(h % RING)

        @block.scalar
        def _(act):
            act.dma_start(dense_sb[:, :, :], dense.rearrange("(p j) f -> p j f", p=P)).then_inc(small_in, 16)
            act.dma_start(last_rows[:, :], tables[:, LAST, :]).then_inc(small_in, 16)
            act.dma_start(wbot_sb[:, 0:NF], w_bot_t).then_inc(small_in, 16)
            act.dma_start(wbot_sb[:, NF:DC], b_bot.rearrange("(d o) -> d o", o=1)).then_inc(small_in, 16)
            act.dma_start(btop_sb[:, :], b_top.rearrange("(d n) -> d n", d=D)).then_inc(small_in, 16)
            act.wait_ge(consts_ready, 1)
            act.activation(warm[:, :], warm[:, :], ACT.Sigmoid)

            def copy_turned(r, q):
                act.wait_ge(turned, r + 1)
                if not isinstance(r, int):
                    act.wait_ge(scored, r - 1)
                act.activation(got_t[:, q, :, :], ps_turn[:, q, :, :], ACT.Copy).then_inc(copied, 1)

            copy_turned(0, 0)
            act.wait_ge(count_ready, 1)
            n = act.value_load(n_rounds[0:1, 0:1], min_val=0, max_val=MAX_ROUNDS)
            with act.Fori(0, MAX_ROUNDS // RING) as i:
                for h in range(1, RING + 1):
                    with act.If(i * RING + h < n):
                        copy_turned(i * RING + h, h % 2)
            act.wait_ge(acc_ready, 1)
            act.activation(prob[:, :], acc[:, :], ACT.Sigmoid).then_inc(prob_ready, 1)

        @block.tensor
        def _(pe):
            pe.wait_ge(consts_ready, 1)
            pe.wait_ge(keys_ready, 1)
            pe.transpose(ps_misc[0:1, 0, 0:P], n_last[:, :], ident[:, :]).then_inc(count_turned, 1)
            pe.wait_ge(small_in, 16 * 5)
            pe.transpose(ps_misc[0:D, 1, 0:T], last_rows[:, :], ident[0:T, 0:T]).then_inc(rows_turned, 1)
            pe.wait_ge(wsum_ready, 1)
            pe.matmul(ps_misc[:, 2, 0:TP], shift[:, 0, :, :], wsum[:, :], start=True, stop=True)
            pe.matmul(ps_misc[:, 2, TP:2 * TP], shift[:, 1, :, :], wsum[:, :], start=True, stop=True).then_inc(w_moved, 1)
            pe.wait_ge(prods_ready, 1)
            pe.matmul(ps_misc[:, 3, 0:T + DC], ones[:, :], prods[:, :], start=True, stop=True).then_inc(coef_ready, 1)

            def multiply(r, b, q, nth):
                pe.wait_ge(gathered[b], SLOTS * 16 * nth)
                for k in range(PAIRS):
                    mm = pe.transpose(ps_turn[:, q, k, :], got[:, b, 2 * k:2 * k + 2, :], ident[:, :])
                mm.then_inc(turned, 1)
                pe.wait_ge(copied, r + 1)
                if not isinstance(r, int):
                    pe.wait_ge(used, r - 1)
                for k in range(PAIRS):
                    mm = pe.matmul(ps_dots[:, q, 2 * T * k:2 * T * (k + 1)], got_t[:, q, k, :], w_blk[:, :, :],
                                   start=True, stop=True)
                mm.then_inc(scored, 1)

            pe.wait_ge(w_ready, 1)
            multiply(0, 0, 0, 1)
            pe.wait_ge(count_ready, 1)
            n = pe.value_load(n_rounds[0:1, 0:1], min_val=0, max_val=MAX_ROUNDS)
            with pe.Fori(0, MAX_ROUNDS // RING) as i:
                for h in range(1, RING + 1):
                    with pe.If(i * RING + h < n):
                        multiply(i * RING + h, h % RING, h % 2, i + 1 + h // RING)

        @block.vector
        def _(v):
            steps = [0]

            def done():
                return steps[0]

            def count(ins):
                steps[0] += 1
                return ins

            v.memset(ones[:, :], 1.0).then_inc(vec, 1)
            v.memset(w_blk[:, :, :], 0.0).then_inc(vec, 1)
            v.wait_ge(iotas_ready, 6)
            v.tensor_scalar(iota_j1[:, :, :], iota_j1[:, :, :], 1.0 / (1 << J_BITS), None, ALU.mult).then_inc(vec, 1)
            v.tensor_scalar(ident[:, :], iota_row[:, :], iota_col[:, :], None, ALU.is_equal).then_inc(vec, 1)
            v.wait_ge(vec, 4)
            v.scalar_tensor_tensor(out=key_base[:, :], in0=iota_t16k[:, :, :].rearrange("p j t -> p (j t)"), scalar=float(1 << ROW_BITS),
                                   in1=iota_j1[:, :, :].rearrange("p j t -> p (j t)"), op0=ALU.mult, op1=ALU.add).then_inc(vec, 1)
            for o in range(2):
                for m in range(2):
                    ins = v.tensor_copy(shift[:, o, m, :], ident[:, o * D:(o + 1) * D])
                    ins.then_inc(vec, 1)
            v.memset(warm[:, :], 1.0).then_inc(consts_ready, 1)

            v.wait_ge(idx_in, 16)
            v.tensor_scalar(wrap[:, :], idx[:, :], 0.0, float(VOCAB), ALU.is_lt, ALU.mult).then_inc(vec, 1)
            v.wait_ge(vec, 10)
            v.tensor_tensor(row[:, :], wrap[:, :], idx[:, :], ALU.add).then_inc(vec, 1)
            v.wait_ge(vec, 11)
            v.scalar_tensor_tensor(out=key_all[:, :], in0=row[:, :], scalar=0.0, in1=key_base[:, :],
                                   op0=ALU.max, op1=ALU.add).then_inc(vec, 1)
            v.wait_ge(vec, 12)
            v.scalar_tensor_tensor(out=keys[:, :], in0=row[:, :], scalar=float(LAST), in1=key_all[:, :],
                                   op0=ALU.is_lt, op1=ALU.mult).then_inc(vec, 1)

            PRE = 13

            def pick(before, b):
                v.max(top[:, b, :], keys[:, :]).then_inc(vec, 1)
                v.wait_ge(vec, before + 1)
                v.tensor_scalar(code[:, b, :], top[:, b, :], float(1 << J_BITS), None, ALU.mult).then_inc(vec, 1)
                v.match_replace(keys[:, :], top[:, b, :], keys[:, :], 0.0).then_inc(vec, 1)
                v.wait_ge(vec, before + 2)
                v.tensor_scalar(tab_row[:, b, :], code[:, b, :], J_BITS, None, ALU.logical_shift_right).then_inc(vec, 1)
                v.tensor_scalar(tab[:, b, :], code[:, b, :], ROW_BITS + J_BITS, None, ALU.logical_shift_right).then_inc(vec, 1)
                v.tensor_scalar(jj[:, b, :], code[:, b, :], (1 << J_BITS) - 1, None, ALU.bitwise_and).then_inc(vec, 1)
                v.wait_ge(vec, before + 5)
                v.scalar_tensor_tensor(out=flat[:, b, :], in0=tab[:, b, :], scalar=float(VOCAB - (1 << ROW_BITS)),
                                       in1=tab_row[:, b, :], op0=ALU.mult, op1=ALU.add).then_inc(flat_ready, 1)

            NPICK = 6

            def masks(b):
                v.tensor_tensor(is_tab[:, :, :], tab[:, b, :, None].broadcast_to([P, SLOTS, T]), iota_t[:, :, :],
                                ALU.is_equal).then_inc(vec, 1)
                v.tensor_tensor(is_j[:, :, :], jj[:, b, None, :].broadcast_to([P, J, SLOTS]), iota_j[:, :, :],
                                ALU.is_equal).then_inc(vec, 1)

            def add_up(r, before, q):
                v.wait_ge(vec, before)
                v.wait_ge(scored, r + 1)
                v.tensor_tensor(picked[:, :, :], is_tab[:, :, :],
                                ps_dots[:, q, 0:SLOTS * T].rearrange("p (s t) -> p s t", s=SLOTS),
                                ALU.mult).then_inc(used, 1)
                v.wait_ge(used, r + 1)
                v.tensor_reduce(dots[:, :], picked[:, :, :], AX.X, ALU.add).then_inc(vec, 1)
                v.wait_ge(vec, before + 1)
                v.tensor_tensor(by_j[:, :, :], is_j[:, :, :], dots[:, None, :].broadcast_to([P, J, SLOTS]),
                                ALU.mult).then_inc(vec, 1)
                v.wait_ge(vec, before + 2)
                v.tensor_reduce(round_sum[:, :], by_j[:, :, :], AX.X, ALU.add).then_inc(vec, 1)
                v.wait_ge(vec, before + 3)
                v.tensor_tensor(acc[:, :], acc[:, :], round_sum[:, :], ALU.add).then_inc(vec, 1)

            NMASK, NADD = 2, 4
            NROUND = NMASK + NPICK + NADD
            v.wait_ge(vec, PRE)
            pick(PRE, 0)
            base = PRE + NPICK
            v.tensor_scalar(at_last[:, :], row[:, :], float(LAST), 0.0, ALU.is_ge, ALU.add,
                            accum_out=n_last[:, :]).then_inc(keys_ready, 1)
            v.wait_ge(vec, base)
            pick(base, 1)
            base += NPICK
            v.wait_ge(count_turned, 1)
            v.tensor_reduce(n_min[:, :], ps_misc[0:1, 0, 0:P], AX.X, ALU.min).then_inc(vec, 1)
            v.wait_ge(vec, base + 1)
            v.tensor_scalar(n_int[:, :], n_min[:, :], -1.0, float(L + SLOTS - 1), ALU.mult, ALU.add).then_inc(vec, 1)
            v.wait_ge(vec, base + 2)
            v.tensor_scalar(n_rounds[:, :], n_int[:, :], SLOTS.bit_length() - 1, None,
                            ALU.logical_shift_right).then_inc(count_ready, 1)
            base += 2

            v.wait_ge(weights_in, 32)
            v.tensor_reduce(wsum[:, :], wt_sb[:, :, :], AX.X, ALU.add).then_inc(wsum_ready, 1)
            v.tensor_reduce(wdsum[:, :], wd_sb[:, :], AX.X, ALU.add).then_inc(vec, 1)
            v.wait_ge(small_in, 16 * 5)
            v.tensor_reduce(bsum[:, :], btop_sb[:, :], AX.X, ALU.add).then_inc(vec, 1)
            v.wait_ge(vec, base + 1)
            v.tensor_scalar(w_dense[:, :], wdsum[:, :], 1.0 / NTOP, None, ALU.mult).then_inc(vec, 1)
            v.wait_ge(w_moved, 1)
            moved = ps_misc[:, 2, 0:T].rearrange("p (o c) -> p c o", o=2)
            v.tensor_scalar(w_blk[0:D, 0, :].rearrange("p (c o) -> p c o", o=2), moved[0:D, :, :], 1.0 / NTOP, None, ALU.mult).then_inc(vec, 1)
            v.tensor_scalar(w_blk[D:P, 1, :].rearrange("p (c o) -> p c o", o=2), moved[D:P, :, :], 1.0 / NTOP, None, ALU.mult).then_inc(w_ready, 1)
            v.wait_ge(rows_turned, 1)
            v.wait_ge(vec, base + 4)
            v.tensor_tensor(prods[:, 0:T], w_blk[0:D, 0, :], ps_misc[0:D, 1, 0:T], ALU.mult).then_inc(vec, 1)
            v.tensor_scalar(prods[:, T:T + DC], wbot_sb[:, :], w_dense[:, :], None, ALU.mult).then_inc(vec, 1)
            v.wait_ge(vec, base + 6)
            v.scalar_tensor_tensor(out=prods[:, T + NF:T + DC], in0=bsum[:, :], scalar=1.0 / NTOP, in1=prods[:, T + NF:T + DC],
                                   op0=ALU.mult, op1=ALU.add).then_inc(prods_ready, 1)
            v.wait_ge(coef_ready, 1)
            v.tensor_copy(coef[:, :], ps_misc[:, 3, 0:T + DC]).then_inc(vec, 1)
            v.wait_ge(vec, base + 7)
            v.tensor_tensor(last_part[:, :, :], at_last[:, :].rearrange("p (j t) -> p j t", j=J),
                            coef[:, None, 0:T].broadcast_to([P, J, T]), ALU.mult).then_inc(vec, 1)
            v.tensor_tensor(dense_part[:, :, :], dense_sb[:, :, :],
                            coef[:, None, T:T + NF].broadcast_to([P, J, NF]), ALU.mult).then_inc(vec, 1)
            v.wait_ge(vec, base + 9)
            v.tensor_reduce(last_sum[:, :], last_part[:, :, :], AX.X, ALU.add).then_inc(vec, 1)
            v.tensor_reduce(dense_sum[:, :], dense_part[:, :, :], AX.X, ALU.add).then_inc(vec, 1)
            v.wait_ge(vec, base + 11)
            v.scalar_tensor_tensor(out=acc[:, :], in0=dense_sum[:, :], scalar=coef[:, T + NF:T + DC], in1=last_sum[:, :],
                                   op0=ALU.add, op1=ALU.add).then_inc(vec, 1)
            base += 12
            v.wait_ge(vec, base)
            masks(0)
            pick(base + NMASK, 2)
            add_up(0, base + NMASK + NPICK, 0)
            v.wait_ge(vec, base + NROUND)
            v.wait_ge(count_ready, 1)
            n = v.value_load(n_rounds[0:1, 0:1], min_val=0, max_val=MAX_ROUNDS)
            round_end = v.alloc_register("round_end")
            v.reg_mov(round_end, base + 2 * NROUND)
            with v.Fori(0, MAX_ROUNDS // RING) as i:
                for h in range(1, RING + 1):
                    r = i * RING + h
                    with v.If(r < n):
                        before = r * NROUND + base
                        masks(h % RING)
                        pick(before + NMASK, (h + 2) % RING)
                        add_up(r, before + NMASK + NPICK, h % 2)
                        v.wait_ge(vec, round_end)
                        v.reg_add(round_end, round_end, NROUND)
            v.nop().then_inc(acc_ready, 1)


def kernel(**inputs):
    import numpy as _np
    import concourse.bacc as _bacc
    from concourse import mybir as _mybir
    from concourse.bass_utils import run_bass_kernel_spmd as _run

    nc = _bacc.Bacc("TRN2", target_bir_lowering=False, num_devices=1)
    given = {
        "dense": inputs["r_dense_features"],
        "sparse": inputs["r_sparse_features"],
        "tables": inputs["L0_rec_tables"],
        "w_bot_t": _np.ascontiguousarray(_np.asarray(inputs["L0_rec_W_bot"]).T),
        "b_bot": inputs["L0_rec_b_bot"],
        "w_top": inputs["L0_rec_W_top"],
        "b_top": inputs["L0_rec_b_top"],
    }
    arrays, args = {}, []
    for name, a in given.items():
        a = _np.ascontiguousarray(a)
        arrays[f"in_{name}"] = a
        args.append(nc.dram_tensor(f"in_{name}", a.shape, _mybir.dt.from_np(a.dtype), kind="ExternalInput").ap())
    batch = arrays["in_dense"].shape[0]
    args.append(nc.dram_tensor("out_prob", (batch,), _mybir.dt.float32, kind="ExternalOutput").ap())
    recommender_head(nc, *args)
    r = _run(nc, [arrays], core_ids=[0])
    return r.results[0]["out_prob"]
```

```python
from contextlib import ExitStack

import concourse.bass as bass
from concourse import mybir

P = 128
F32 = mybir.dt.float32
I32 = mybir.dt.int32
U32 = mybir.dt.uint32
ALU = mybir.AluOpType
ACT = mybir.ActivationFunctionType
AX = mybir.AxisListType

SLOTS = 8
RING = 4
ROW_BITS = 14
J_BITS = 5
NOTHING = float(1 << 20)


def recommender_head(nc, dense, sparse, tables, w_bot_t, b_bot, w_top, b_top, out):
    T, VOCAB, D = tables.shape
    B, NF = dense.shape
    NTOP = w_top.shape[1]
    J = B // P
    L = J * T
    OWN = RING * SLOTS
    MAX_ROUNDS = L // SLOTS
    LAST = VOCAB - 1
    PAIRS = SLOTS // 2
    TP = T // 2
    DC = NF + 1
    TURNS = MAX_ROUNDS // RING
    FEW = 4
    IDLE = float(((T - 1) << ROW_BITS) + LAST)
    assert B % P == 0 and D == 64 and T % 2 == 0 and L % SLOTS == 0
    assert VOCAB < 1 << ROW_BITS and J < (1 << J_BITS) - 1
    assert T << (ROW_BITS + J_BITS) <= 1 << 24 and NOTHING > 2 * IDLE
    assert MAX_ROUNDS % RING == 0 and (TURNS - 1) % FEW == 0

    table_rows = tables.rearrange("t v d -> (t v) d")
    lookup_rows = sparse.rearrange("(p j) t -> p (j t)", p=P)

    with ExitStack() as ctx:
        def sb(name, shape, dt=F32):
            return ctx.enter_context(nc.sbuf_tensor(name, shape, dt))

        def psum(name, shape):
            return ctx.enter_context(nc.psum_tensor(name, shape, F32))

        def sem(name):
            return ctx.enter_context(nc.semaphore(name))

        idx = sb("idx", [P, L], I32)
        idx_partner = sb("idx_partner", [P, L], I32)
        dense_sb = sb("dense_sb", [P, J, NF])
        wt_sb = sb("wt_sb", [P, TP, NTOP])
        wd_sb = sb("wd_sb", [D, NTOP])
        last_rows = sb("last_rows", [T, D])
        wbot_sb = sb("wbot_sb", [D, DC])
        btop_sb = sb("btop_sb", [D, NTOP // D])
        table_base = sb("table_base", [P, J, T])
        j_base = sb("j_base", [P, J, T])
        iota_t = sb("iota_t", [P, SLOTS, T])
        iota_j = sb("iota_j", [P, 2, J, SLOTS])
        iota_col = sb("iota_col", [P, P])
        iota_row = sb("iota_row", [P, 1])
        iota_mix = sb("iota_mix", [P, 1])
        iota_slot = sb("iota_slot", [P, SLOTS])
        ident = sb("ident", [P, P])
        shift = sb("shift", [P, 2, 2, D])
        ones = sb("ones", [P, P])
        key_base = sb("key_base", [P, L])
        wrap = sb("wrap", [P, L])
        row = sb("row", [P, L])
        key_all = sb("key_all", [P, L])
        keys = sb("keys", [P, 2, L])
        at_last = sb("at_last", [P, L])
        partner_last = sb("partner_last", [P, L])
        n_last = sb("n_last", [P, 1])
        n_partner_last = sb("n_partner_last", [P, 1])
        mix = sb("mix", [P, 1])
        n_own = sb("n_own", [P, 1])
        diag = sb("diag", [P, 3, P])
        greater = sb("greater", [P, P])
        rank = sb("rank", [P, 1])
        pair = sb("pair", [P, P])
        pair_mix = sb("pair_mix", [P, P])
        mix_partner = sb("mix_partner", [P, 1])
        mix_int = sb("mix_int", [P, 1], U32)
        n_partner = sb("n_partner", [P, 1], U32)
        partner = sb("partner", [P, 1], U32)
        n_partner_f = sb("n_partner_f", [P, 1])
        own_1 = sb("own_1", [P, 1])
        own_slots = sb("own_slots", [P, 1])
        pair_sum = sb("pair_sum", [P, 1], I32)
        pair_mean_f = sb("pair_mean_f", [P, 1])
        pair_mean = sb("pair_mean", [P, 1], I32)
        n_slots_f = sb("n_slots_f", [P, 1])
        n_slots = sb("n_slots", [P, 1], I32)
        from_partner = sb("from_partner", [P, 1])
        quota = sb("quota", [P, 1])
        left = sb("left", [P, SLOTS])
        top = sb("top", [P, RING, SLOTS])
        size = sb("size", [P, RING, SLOTS])
        code = sb("code", [P, RING, SLOTS], I32)
        tab_row = sb("tab_row", [P, RING, SLOTS], I32)
        tab = sb("tab", [P, RING, SLOTS], I32)
        j_code = sb("j_code", [P, RING, SLOTS], I32)
        side = sb("side", [P, RING, SLOTS])
        j_side = sb("j_side", [P, RING, SLOTS])
        j_of = sb("j_of", [P, RING, SLOTS])
        flat = sb("flat", [P, RING, SLOTS], U32)
        got = sb("got", [P, RING, SLOTS, D])
        got_t = sb("got_t", [P, 2, PAIRS, P])
        is_tab = sb("is_tab", [P, SLOTS, T])
        picked = sb("picked", [P, SLOTS, T])
        dots = sb("dots", [P, SLOTS])
        is_j = sb("is_j", [P, 2 * J, SLOTS])
        by_j = sb("by_j", [P, 2 * J, SLOTS])
        round_sum = sb("round_sum", [P, 2 * J])
        acc = sb("acc", [P, 2 * J])
        wsum = sb("wsum", [P, TP])
        wdsum = sb("wdsum", [D, 1])
        w_blk = sb("w_blk", [P, 2, T])
        w_dense = sb("w_dense", [D, 1])
        bsum = sb("bsum", [D, 1])
        prods = sb("prods", [D, T + DC])
        coef = sb("coef", [P, T + DC])
        last_part = sb("last_part", [P, J, T])
        dense_part = sb("dense_part", [P, J, NF])
        last_sum = sb("last_sum", [P, J])
        dense_sum = sb("dense_sum", [P, J])
        warm = sb("warm", [1, 1])
        logit = sb("logit", [P, J])
        prob = sb("prob", [P, J])

        ps_turn = psum("ps_turn", [P, 2, PAIRS, P])
        ps_dots = psum("ps_dots", [P, 2, 512])
        ps_pair = psum("ps_pair", [P, 4, P])
        ps_rows = psum("ps_rows", [D, 512])
        ps_w = psum("ps_w", [P, 512])
        ps_coef = psum("ps_coef", [P, 512])

        idx_in = sem("idx_in")
        partner_in = sem("partner_in")
        weights_in = sem("weights_in")
        small_in = sem("small_in")
        iotas_ready = sem("iotas_ready")
        vec = sem("vec")
        vec_pick = sem("vec_pick")
        vec_sum = sem("vec_sum")
        consts_ready = sem("consts_ready")
        diag_ready = sem("diag_ready")
        spread = sem("spread")
        partner_ready = sem("partner_ready")
        slots_ready = sem("slots_ready")
        wsum_ready = sem("wsum_ready")
        w_moved = sem("w_moved")
        w_ready = sem("w_ready")
        rows_turned = sem("rows_turned")
        prods_ready = sem("prods_ready")
        coef_ready = sem("coef_ready")
        flat_ready = sem("flat_ready")
        gathered = [sem(f"gathered{b}") for b in range(RING)]
        turned = sem("turned")
        copied = sem("copied")
        scored = sem("scored")
        used = sem("used")
        swapped = sem("swapped")
        logit_ready = sem("logit_ready")
        prob_ready = sem("prob_ready")
        stored = sem("stored")

        block = ctx.enter_context(nc.Block())

        NSUM = 6
        NPICK_OWN = 8
        NPICK = 11

        def ring_turns(eng, rounds, one_round):
            with eng.Fori(0, (TURNS - 1) // FEW) as few:
                with eng.If(few * (FEW * RING) + RING < rounds):
                    with eng.Fori(0, FEW) as one:
                        turn = eng.snap(few * FEW + one + 1, min_val=1, max_val=TURNS - 1)
                        with eng.If(turn * RING < rounds):
                            for h in range(RING):
                                with eng.If(turn * RING + h < rounds):
                                    one_round(turn, h)

        def load_slots(eng):
            eng.wait_ge(slots_ready, 1)
            n = eng.value_load(n_slots[0:1, 0:1], min_val=OWN, max_val=L)
            return n, eng.snap((n + SLOTS - 1) // SLOTS, min_val=RING, max_val=MAX_ROUNDS)

        @block.sync
        def _(sp):
            sp.dma_start(idx[:, :], lookup_rows).then_inc(idx_in, 16)
            sp.dma_start(wt_sb[:, :, :], w_top[0:T * D, :].rearrange("(c q) n -> q c n", q=P)).then_inc(weights_in, 16)
            sp.dma_start(wd_sb[:, :], w_top[T * D:T * D + D, :]).then_inc(weights_in, 16)
            sp.wait_ge(prob_ready, 1)
            sp.dma_start(out.rearrange("(p j) -> p j", p=P), prob[:, :]).then_inc(stored, 16)
            sp.wait_ge(stored, 16)

        @block.gpsimd
        def _(pool):
            def iota(tile, pattern, base=0, per_partition=0):
                pool.iota(tile, pattern, base=base, channel_multiplier=per_partition,
                          allow_small_or_imprecise_dtypes=True).then_inc(iotas_ready, 1)

            iota(table_base[:, :, :], [[0, J], [1, T]])
            iota(j_base[:, :, :], [[1, J], [0, T]], base=1)
            iota(iota_col[:, :], [[1, P]])
            iota(iota_row[:, :], [[0, 1]], per_partition=1)
            iota(iota_mix[:, :], [[0, 1]], base=L * P, per_partition=1)
            iota(iota_t[:, :, :], [[0, SLOTS], [1, T]])
            iota(iota_j[:, 0, :, :], [[1, J], [0, SLOTS]], base=1)
            iota(iota_j[:, 1, :, :], [[-1, J], [0, SLOTS]], base=-1)
            iota(iota_slot[:, :], [[-1, SLOTS]], base=-OWN)

            due = pool.alloc_register("due")
            pool.reg_mov(due, 1)

            def gather(b, s):
                pool.indirect_dma_start(
                    got[:, b, s, :], None, table_rows,
                    bass.IndirectOffsetOnAxis(ap=flat[:, b, s:s + 1], axis=0),
                ).then_inc(gathered[b], 16)

            for b in range(RING):
                pool.wait_ge(flat_ready, b + 1)
                for s in range(SLOTS):
                    gather(b, s)
                if b == 0:
                    pool.wait_ge(partner_ready, 1)
                    pool.indirect_dma_start(
                        idx_partner[:, :], None, lookup_rows,
                        bass.IndirectOffsetOnAxis(ap=partner[:, 0:1], axis=0),
                    ).then_inc(partner_in, 16)
            n, rounds = load_slots(pool)
            pool.reg_mov(due, RING + 1)

            def gather_round(turn, b):
                pool.wait_ge(flat_ready, due)
                pool.reg_add(due, due, 1)
                first = (turn * RING + b) * SLOTS
                with pool.If(first + SLOTS <= n):
                    for s in range(SLOTS):
                        gather(b, s)
                with pool.Else():
                    for s in range(SLOTS - 1):
                        with pool.If(first + s < n):
                            gather(b, s)

            ring_turns(pool, rounds, gather_round)

        @block.scalar
        def _(act):
            act.dma_start(dense_sb[:, :, :], dense.rearrange("(p j) f -> p j f", p=P)).then_inc(small_in, 16)
            act.dma_start(last_rows[:, :], tables[:, LAST, :]).then_inc(small_in, 16)
            act.dma_start(wbot_sb[:, 0:NF], w_bot_t).then_inc(small_in, 16)
            act.dma_start(wbot_sb[:, NF:DC], b_bot.rearrange("(d o) -> d o", o=1)).then_inc(small_in, 16)
            act.dma_start(btop_sb[:, :], b_top.rearrange("(d n) -> d n", d=D)).then_inc(small_in, 16)
            act.wait_ge(consts_ready, 1)
            act.activation(warm[:, :], warm[:, :], ACT.Sigmoid)

            def copy_turned(r, q):
                act.wait_ge(turned, r + 1)
                act.activation(got_t[:, q, :, :], ps_turn[:, q, :, :], ACT.Copy).then_inc(copied, 1)

            for r in range(RING):
                if r >= 2:
                    act.wait_ge(scored, r - 1)
                copy_turned(r, r % 2)
            n, rounds = load_slots(act)

            def copy_round(turn, h):
                act.wait_ge(scored, turn * RING + (h - 1))
                copy_turned(turn * RING + h, h % 2)

            ring_turns(act, rounds, copy_round)
            act.wait_ge(logit_ready, 1)
            act.activation(prob[:, :], logit[:, :], ACT.Sigmoid).then_inc(prob_ready, 1)

        @block.tensor
        def _(pe):
            def spread_diag(k):
                pe.wait_ge(diag_ready, k + 1)
                pe.matmul(ps_pair[:, k, :], ones[:, :], diag[:, k, :], start=True, stop=True).then_inc(spread, 1)

            pe.wait_ge(consts_ready, 1)
            spread_diag(0)
            spread_diag(1)
            spread_diag(2)
            pe.wait_ge(small_in, 16 * 5)
            pe.transpose(ps_rows[:, 0:T], last_rows[:, :], ident[0:T, 0:T]).then_inc(rows_turned, 1)
            pe.wait_ge(wsum_ready, 1)
            pe.matmul(ps_w[:, 0:TP], shift[:, 0, :, :], wsum[:, :], start=True, stop=True)
            pe.matmul(ps_w[:, TP:2 * TP], shift[:, 1, :, :], wsum[:, :], start=True, stop=True).then_inc(w_moved, 1)
            pe.wait_ge(prods_ready, 1)
            pe.matmul(ps_coef[:, 0:T + DC], ones[0:D, :], prods[:, :], start=True, stop=True).then_inc(coef_ready, 1)

            def turn_rows(b, q, landed):
                pe.wait_ge(gathered[b], landed)
                for k in range(PAIRS):
                    mm = pe.transpose(ps_turn[:, q, k, :], got[:, b, 2 * k:2 * k + 2, :], ident[:, :])
                mm.then_inc(turned, 1)

            def multiply(r, q):
                pe.wait_ge(copied, r + 1)
                for k in range(PAIRS):
                    mm = pe.matmul(ps_dots[:, q, 2 * T * k:2 * T * (k + 1)], got_t[:, q, k, :], w_blk[:, :, :],
                                   start=True, stop=True)
                mm.then_inc(scored, 1)

            pe.wait_ge(w_ready, 1)
            for r in range(RING):
                turn_rows(r, r % 2, SLOTS * 16)
                if r >= 2:
                    pe.wait_ge(used, r - 1)
                multiply(r, r % 2)
            n, rounds = load_slots(pe)

            at_most = pe.alloc_register("at_most")
            slots = pe.alloc_register("slots")

            def multiply_round(turn, h):
                pe.reg_alu(at_most, n - (turn * RING + h) * SLOTS, SLOTS, op=ALU.min)
                pe.reg_alu(slots, at_most, 1, op=ALU.max)
                here = pe.snap(slots, min_val=1, max_val=SLOTS)
                turn_rows(h, h % 2, turn * (SLOTS * 16) + here * 16)
                pe.wait_ge(used, turn * RING + (h - 1))
                multiply(turn * RING + h, h % 2)

            ring_turns(pe, rounds, multiply_round)
            pe.wait_ge(vec_sum, rounds * NSUM)
            pe.matmul(ps_pair[:, 3, 0:J], pair[:, :], acc[:, J:2 * J], start=True, stop=True).then_inc(swapped, 1)

        @block.vector
        def _(v):
            v.memset(ones[:, :], 1.0).then_inc(vec, 1)
            v.memset(w_blk[:, :, :], 0.0).then_inc(vec, 1)
            v.memset(acc[:, :], 0.0).then_inc(vec, 1)
            v.memset(warm[:, :], 1.0).then_inc(vec, 1)
            v.wait_ge(iotas_ready, 2)
            v.tensor_scalar(j_base[:, :, :], j_base[:, :, :], 1.0 / (1 << J_BITS), None, ALU.mult).then_inc(vec, 1)
            v.wait_ge(vec, 5)
            v.scalar_tensor_tensor(out=key_base[:, :], in0=table_base[:, :, :].rearrange("p j t -> p (j t)"),
                                   scalar=float(1 << ROW_BITS), in1=j_base[:, :, :].rearrange("p j t -> p (j t)"),
                                   op0=ALU.mult, op1=ALU.add).then_inc(vec, 1)
            v.wait_ge(iotas_ready, 4)
            v.tensor_scalar(ident[:, :], iota_col[:, :], iota_row[:, :], None, ALU.is_equal).then_inc(consts_ready, 1)

            def read_keys(at, before, indices, last, n):
                v.tensor_scalar(wrap[:, :], indices[:, :], 0.0, float(VOCAB), ALU.is_lt, ALU.mult).then_inc(vec, 1)
                v.wait_ge(vec, before + 1)
                v.tensor_tensor(row[:, :], wrap[:, :], indices[:, :], ALU.add).then_inc(vec, 1)
                v.wait_ge(vec, before + 2)
                v.scalar_tensor_tensor(out=key_all[:, :], in0=row[:, :], scalar=0.0, in1=key_base[:, :],
                                       op0=ALU.max, op1=ALU.add).then_inc(vec, 1)
                v.tensor_scalar(last[:, :], row[:, :], float(LAST), 0.0, ALU.is_ge, ALU.add,
                                accum_out=n[:, :]).then_inc(vec, 1)
                v.wait_ge(vec, before + 4)
                v.scalar_tensor_tensor(out=keys[:, at, :], in0=last[:, :], scalar=-NOTHING, in1=key_all[:, :],
                                       op0=ALU.mult, op1=ALU.subtract if at else ALU.add).then_inc(vec, 1)

            v.wait_ge(idx_in, 16)
            read_keys(0, 6, idx, at_last, n_last)
            v.wait_ge(vec, 11)

            def pick(before, b, partners):
                candidates = keys[:, :, :].rearrange("p o l -> p (o l)") if partners else keys[:, 0, :]
                v.max(top[:, b, :], candidates).then_inc(vec_pick, 1)
                v.wait_ge(vec_pick, before + 1)
                v.scalar_tensor_tensor(out=size[:, b, :], in0=top[:, b, :], scalar=-1.0, in1=top[:, b, :],
                                       op0=ALU.mult, op1=ALU.max).then_inc(vec_pick, 1)
                v.wait_ge(vec_pick, before + 2)
                v.tensor_scalar(code[:, b, :], size[:, b, :], IDLE, float(1 << J_BITS), ALU.min,
                                ALU.mult).then_inc(vec_pick, 1)
                v.wait_ge(vec_pick, before + 3)
                v.tensor_scalar(tab[:, b, :], code[:, b, :], ROW_BITS + J_BITS, None,
                                ALU.logical_shift_right).then_inc(vec_pick, 1)
                v.tensor_scalar(tab_row[:, b, :], code[:, b, :], J_BITS, None,
                                ALU.logical_shift_right).then_inc(vec_pick, 1)
                v.wait_ge(vec_pick, before + 5)
                v.scalar_tensor_tensor(out=flat[:, b, :], in0=tab[:, b, :], scalar=float(VOCAB - (1 << ROW_BITS)),
                                       in1=tab_row[:, b, :], op0=ALU.mult, op1=ALU.add).then_inc(flat_ready, 1)
                v.match_replace(candidates, top[:, b, :], candidates, -NOTHING).then_inc(vec_pick, 1)
                v.tensor_scalar(j_code[:, b, :], code[:, b, :], (1 << J_BITS) - 1, None,
                                ALU.bitwise_and).then_inc(vec_pick, 1)
                if not partners:
                    v.wait_ge(vec_pick, before + 7)
                    v.tensor_copy(j_of[:, b, :], j_code[:, b, :]).then_inc(vec_pick, 1)
                    return
                v.tensor_scalar(side[:, b, :], top[:, b, :], 0.0, -2.0, ALU.is_lt, ALU.mult).then_inc(vec_pick, 1)
                v.wait_ge(vec_pick, before + 8)
                v.scalar_tensor_tensor(out=j_side[:, b, :], in0=side[:, b, :], scalar=1.0, in1=j_code[:, b, :],
                                       op0=ALU.add, op1=ALU.mult).then_inc(vec_pick, 1)
                v.wait_ge(vec_pick, before + 9)
                v.scalar_tensor_tensor(out=j_of[:, b, :], in0=left[:, :], scalar=0.0, in1=j_side[:, b, :],
                                       op0=ALU.is_gt, op1=ALU.mult).then_inc(vec_pick, 1)
                v.tensor_scalar(left[:, :], left[:, :], -float(SLOTS), None, ALU.add).then_inc(vec_pick, 1)

            def add_up(r, picks, b, q):
                before = r * NSUM
                v.wait_ge(vec_pick, picks)
                v.tensor_tensor(is_tab[:, :, :], tab[:, b, :, None].broadcast_to([P, SLOTS, T]), iota_t[:, :, :],
                                ALU.is_equal).then_inc(vec_sum, 1)
                v.tensor_tensor(is_j[:, :, :], j_of[:, b, None, :].broadcast_to([P, 2 * J, SLOTS]),
                                iota_j[:, :, :, :].rearrange("p o j s -> p (o j) s"), ALU.is_equal).then_inc(vec_sum, 1)
                v.wait_ge(vec_sum, before + 1)
                v.wait_ge(scored, r + 1)
                v.tensor_tensor(picked[:, :, :], is_tab[:, :, :],
                                ps_dots[:, q, 0:SLOTS * T].rearrange("p (s t) -> p s t", s=SLOTS),
                                ALU.mult).then_inc(used, 1)
                v.wait_ge(used, r + 1)
                v.tensor_reduce(dots[:, :], picked[:, :, :], AX.X, ALU.add).then_inc(vec_sum, 1)
                v.wait_ge(vec_sum, before + 3)
                v.tensor_tensor(by_j[:, :, :], is_j[:, :, :], dots[:, None, :].broadcast_to([P, 2 * J, SLOTS]),
                                ALU.mult).then_inc(vec_sum, 1)
                v.wait_ge(vec_sum, before + 4)
                v.tensor_reduce(round_sum[:, :], by_j[:, :, :], AX.X, ALU.add).then_inc(vec_sum, 1)
                v.wait_ge(vec_sum, before + 5)
                v.tensor_tensor(acc[:, :], acc[:, :], round_sum[:, :], ALU.add).then_inc(vec_sum, 1)

            pick(0, 0, False)

            v.wait_ge(iotas_ready, 9)
            v.tensor_scalar(mix[:, :], n_last[:, :], -float(P), iota_mix[:, :], ALU.mult, ALU.add).then_inc(vec, 1)
            v.tensor_scalar(n_own[:, :], n_last[:, :], -1.0, float(L), ALU.mult, ALU.add).then_inc(vec, 1)
            v.wait_ge(vec, 12)
            v.wait_ge(consts_ready, 1)
            v.tensor_scalar(diag[:, 0, :], ident[:, :], mix[:, :], None, ALU.mult).then_inc(diag_ready, 1)
            for o in range(2):
                for m in range(2):
                    v.tensor_copy(shift[:, o, m, :], ident[:, o * D:(o + 1) * D]).then_inc(vec, 1)
            pick(NPICK_OWN, 1, False)
            v.wait_ge(spread, 1)
            v.tensor_scalar(greater[:, :], ps_pair[:, 0, :], mix[:, :], 0.0, ALU.is_gt, ALU.add,
                            accum_out=rank[:, :]).then_inc(vec, 1)
            v.wait_ge(vec, 18)
            v.tensor_scalar(diag[:, 1, :], ident[:, :], rank[:, :], None, ALU.mult).then_inc(diag_ready, 1)
            pick(2 * NPICK_OWN, 2, False)
            v.wait_ge(spread, 2)
            v.tensor_scalar(pair[:, :], ps_pair[:, 1, :], rank[:, :], float(P - 1), ALU.add, ALU.is_equal).then_inc(vec, 1)
            v.wait_ge(vec, 19)
            v.tensor_tensor(pair_mix[:, :], pair[:, :], ps_pair[:, 0, :], ALU.mult).then_inc(vec, 1)
            v.wait_ge(vec, 20)
            v.tensor_reduce(mix_partner[:, :], pair_mix[:, :], AX.X, ALU.add).then_inc(vec, 1)
            v.wait_ge(vec, 21)
            v.tensor_copy(mix_int[:, :], mix_partner[:, :]).then_inc(vec, 1)
            v.wait_ge(vec, 22)
            v.tensor_scalar(partner[:, :], mix_int[:, :], P - 1, None, ALU.bitwise_and).then_inc(partner_ready, 1)
            v.tensor_scalar(n_partner[:, :], mix_int[:, :], P.bit_length() - 1, None,
                            ALU.logical_shift_right).then_inc(vec, 1)
            v.tensor_scalar(own_slots[:, :], n_own[:, :], float(OWN), None, ALU.max).then_inc(vec, 1)
            v.wait_ge(vec, 24)
            v.tensor_scalar(own_1[:, :], own_slots[:, :], 1.0, None, ALU.add).then_inc(vec, 1)
            v.tensor_copy(n_partner_f[:, :], n_partner[:, :]).then_inc(vec, 1)
            v.wait_ge(vec, 26)
            v.scalar_tensor_tensor(out=pair_sum[:, :], in0=n_partner_f[:, :], scalar=float(OWN), in1=own_1[:, :],
                                   op0=ALU.max, op1=ALU.add).then_inc(vec, 1)
            v.wait_ge(vec, 27)
            v.tensor_scalar(pair_mean[:, :], pair_sum[:, :], 1, None, ALU.logical_shift_right).then_inc(vec, 1)
            v.wait_ge(vec, 28)
            v.tensor_copy(pair_mean_f[:, :], pair_mean[:, :]).then_inc(vec, 1)
            v.wait_ge(vec, 29)
            v.tensor_scalar(diag[:, 2, :], ident[:, :], pair_mean_f[:, :], None, ALU.mult).then_inc(diag_ready, 1)
            pick(3 * NPICK_OWN, 3, False)
            v.wait_ge(spread, 3)
            v.tensor_reduce(n_slots_f[:, :], ps_pair[:, 2, :], AX.X, ALU.max).then_inc(vec, 1)
            v.wait_ge(vec, 30)
            v.tensor_copy(n_slots[:, :], n_slots_f[:, :]).then_inc(slots_ready, 1)
            v.tensor_scalar(from_partner[:, :], n_partner_f[:, :], n_slots_f[:, :], 0.0,
                            ALU.subtract, ALU.max).then_inc(vec, 1)
            v.wait_ge(vec, 31)
            v.tensor_scalar(quota[:, :], from_partner[:, :], own_slots[:, :], n_slots_f[:, :],
                            ALU.add, ALU.min).then_inc(vec, 1)
            v.wait_ge(vec, 32)
            v.tensor_scalar(left[:, :], iota_slot[:, :], quota[:, :], None, ALU.add).then_inc(vec, 1)

            v.wait_ge(weights_in, 32)
            v.tensor_reduce(wsum[:, :], wt_sb[:, :, :], AX.X, ALU.add).then_inc(wsum_ready, 1)
            v.tensor_reduce(wdsum[:, :], wd_sb[:, :], AX.X, ALU.add).then_inc(vec, 1)
            v.wait_ge(small_in, 16 * 5)
            v.tensor_reduce(bsum[:, :], btop_sb[:, :], AX.X, ALU.add).then_inc(vec, 1)
            v.wait_ge(vec, 34)
            v.tensor_scalar(w_dense[:, :], wdsum[:, :], 1.0 / NTOP, None, ALU.mult).then_inc(vec, 1)
            v.wait_ge(w_moved, 1)
            moved = ps_w[:, 0:T].rearrange("p (o c) -> p c o", o=2)
            v.tensor_scalar(w_blk[0:D, 0, :].rearrange("p (c o) -> p c o", o=2), moved[0:D, :, :], 1.0 / NTOP, None,
                            ALU.mult).then_inc(vec, 1)
            v.tensor_scalar(w_blk[D:P, 1, :].rearrange("p (c o) -> p c o", o=2), moved[D:P, :, :], 1.0 / NTOP, None,
                            ALU.mult).then_inc(w_ready, 1)
            v.wait_ge(rows_turned, 1)
            v.wait_ge(vec, 37)
            v.tensor_tensor(prods[:, 0:T], w_blk[0:D, 0, :], ps_rows[:, 0:T], ALU.mult).then_inc(vec, 1)
            v.tensor_scalar(prods[:, T:T + DC], wbot_sb[:, :], w_dense[:, :], None, ALU.mult).then_inc(vec, 1)
            v.wait_ge(vec, 39)
            v.scalar_tensor_tensor(out=prods[:, T + NF:T + DC], in0=bsum[:, :], scalar=1.0 / NTOP,
                                   in1=prods[:, T + NF:T + DC], op0=ALU.mult, op1=ALU.add).then_inc(prods_ready, 1)
            v.wait_ge(partner_in, 16)
            read_keys(1, 39, idx_partner, partner_last, n_partner_last)
            v.wait_ge(coef_ready, 1)
            v.tensor_copy(coef[:, :], ps_coef[:, 0:T + DC]).then_inc(vec, 1)
            v.wait_ge(vec, 45)
            v.tensor_tensor(last_part[:, :, :], at_last[:, :].rearrange("p (j t) -> p j t", j=J),
                            coef[:, None, 0:T].broadcast_to([P, J, T]), ALU.mult).then_inc(vec, 1)
            v.tensor_tensor(dense_part[:, :, :], dense_sb[:, :, :],
                            coef[:, None, T:T + NF].broadcast_to([P, J, NF]), ALU.mult).then_inc(vec, 1)
            v.wait_ge(vec, 47)
            v.tensor_reduce(last_sum[:, :], last_part[:, :, :], AX.X, ALU.add).then_inc(vec, 1)
            v.tensor_reduce(dense_sum[:, :], dense_part[:, :, :], AX.X, ALU.add).then_inc(vec, 1)
            v.wait_ge(vec, 49)
            v.scalar_tensor_tensor(out=acc[:, 0:J], in0=dense_sum[:, :], scalar=coef[:, T + NF:T + DC], in1=last_sum[:, :],
                                   op0=ALU.add, op1=ALU.add).then_inc(vec, 1)
            v.wait_ge(vec, 50)

            for r in range(RING):
                add_up(r, (r + 1) * NPICK_OWN, r, r % 2)
                pick(RING * NPICK_OWN + r * NPICK, r, True)
            n, rounds = load_slots(v)

            def sum_round(turn, h):
                r = turn * RING + h
                picked_before = RING * NPICK_OWN + (r - RING) * NPICK
                add_up(r, picked_before + NPICK, h, h % 2)
                with v.If(r + RING < rounds):
                    pick(picked_before + RING * NPICK, h, True)

            ring_turns(v, rounds, sum_round)
            v.wait_ge(swapped, 1)
            v.tensor_tensor(logit[:, :], acc[:, 0:J], ps_pair[:, 3, 0:J], ALU.add).then_inc(logit_ready, 1)


def kernel(**inputs):
    import numpy as _np
    import concourse.bacc as _bacc
    from concourse import mybir as _mybir
    from concourse.bass_utils import run_bass_kernel_spmd as _run

    nc = _bacc.Bacc("TRN2", target_bir_lowering=False, num_devices=1)
    given = {
        "dense": inputs["r_dense_features"],
        "sparse": inputs["r_sparse_features"],
        "tables": inputs["L0_rec_tables"],
        "w_bot_t": _np.ascontiguousarray(_np.asarray(inputs["L0_rec_W_bot"]).T),
        "b_bot": inputs["L0_rec_b_bot"],
        "w_top": inputs["L0_rec_W_top"],
        "b_top": inputs["L0_rec_b_top"],
    }
    arrays, args = {}, []
    for name, a in given.items():
        a = _np.ascontiguousarray(a)
        arrays[f"in_{name}"] = a
        args.append(nc.dram_tensor(f"in_{name}", a.shape, _mybir.dt.from_np(a.dtype), kind="ExternalInput").ap())
    batch = arrays["in_dense"].shape[0]
    args.append(nc.dram_tensor("out_prob", (batch,), _mybir.dt.float32, kind="ExternalOutput").ap())
    recommender_head(nc, *args)
    r = _run(nc, [arrays], core_ids=[0])
    return r.results[0]["out_prob"]
```

```python
from contextlib import ExitStack

import concourse.bass as bass
from concourse import mybir

P = 128
F32 = mybir.dt.float32
I32 = mybir.dt.int32
U32 = mybir.dt.uint32
ALU = mybir.AluOpType
ACT = mybir.ActivationFunctionType
AX = mybir.AxisListType

SLOTS = 8
RING = 4
SPANS = (8, 4, 2, 1)
ROW_BITS = 14
TAB_BITS = 5
KEY_BITS = 24
NOTHING = float(1 << 25)
NO_KEY = float(1 << 27)


def recommender_head(nc, dense, sparse, tables, w_bot_t, b_bot, w_top, b_top, out):
    T, VOCAB, D = tables.shape
    B, NF = dense.shape
    NTOP = w_top.shape[1]
    J = B // P
    L = J * T
    OWN = RING * SLOTS
    MAX_ROUNDS = L // SLOTS
    LAST = VOCAB - 1
    TPAD = 32
    QUADS = P // TPAD
    HALVES = SLOTS // QUADS
    FIRST = 2
    REST = J - FIRST
    J_SHIFT = ROW_BITS + TAB_BITS
    TP = T // 2
    DC = NF + 1
    MIN_FULL = 2 * RING
    LAST_ROUND = RING
    IDLE = float((J << J_SHIFT) + ((T - 1) << ROW_BITS) + LAST)
    assert B % P == 0 and D == 64 and T % 2 == 0 and T <= TPAD and L % SLOTS == 0
    assert FIRST * T >= SLOTS
    assert VOCAB < 1 << ROW_BITS and T <= 1 << TAB_BITS
    assert IDLE < 1 << KEY_BITS and NOTHING > 2 * IDLE
    assert MAX_ROUNDS - 1 - RING < (sum(SPANS) + 1) * RING and 3 * NOTHING < NO_KEY

    table_rows = tables.rearrange("t v d -> (t v) d")

    with ExitStack() as ctx:
        def sb(name, shape, dt=F32):
            return ctx.enter_context(nc.sbuf_tensor(name, shape, dt))

        def psum(name, shape):
            return ctx.enter_context(nc.psum_tensor(name, shape, F32))

        def sem(name):
            return ctx.enter_context(nc.semaphore(name))

        idx = sb("idx", [P, J, T], I32)
        dense_sb = sb("dense_sb", [P, J, NF])
        wt_sb = sb("wt_sb", [P, TP, NTOP])
        wd_sb = sb("wd_sb", [D, NTOP])
        last_rows = sb("last_rows", [T, D])
        wbot_sb = sb("wbot_sb", [D, DC])
        btop_sb = sb("btop_sb", [D, NTOP // D])
        iota_t = sb("iota_t", [P, TPAD])
        iota_j = sb("iota_j", [P, 2, J])
        iota_col = sb("iota_col", [P, P])
        iota_row = sb("iota_row", [P, 1])
        iota_slot = sb("iota_slot", [P, SLOTS])
        j_part = sb("j_part", [P, J])
        ident = sb("ident", [P, P])
        ones = sb("ones", [P, P])
        key_base = sb("key_base", [P, J, T])
        wrap = sb("wrap", [P, J, T])
        row = sb("row", [P, J, T])
        key_all = sb("key_all", [P, J, T])
        keys_row = sb("keys_row", [P, 2 * L + SLOTS])
        keys = keys_row[:, 0:2 * L].rearrange("p (o j t) -> p o j t", o=2, j=J)
        at_last = sb("at_last", [P, J, T])
        partner_last = sb("partner_last", [P, J, T])
        n_last = sb("n_last", [P, 2])
        missed = sb("missed", [P, 1])
        n_last_all = sb("n_last_all", [P, 1])
        n_minus = sb("n_minus", [P, 1])
        n_own = sb("n_own", [P, 1])
        mix = sb("mix", [P, 1])
        diag = sb("diag", [P, 3, P])
        greater = sb("greater", [P, P])
        rank = sb("rank", [P, 1])
        pair = sb("pair", [P, P])
        pair_mix = sb("pair_mix", [P, P])
        mix_partner = sb("mix_partner", [P, 1])
        mix_int = sb("mix_int", [P, 1], U32)
        n_partner = sb("n_partner", [P, 1], U32)
        n_partner_f = sb("n_partner_f", [P, 1])
        own_1 = sb("own_1", [P, 1])
        own_slots = sb("own_slots", [P, 1])
        pair_sum = sb("pair_sum", [P, 1], I32)
        pair_mean_f = sb("pair_mean_f", [P, 1])
        pair_mean = sb("pair_mean", [P, 1], I32)
        n_slots_f = sb("n_slots_f", [P, 1])
        n_slots = sb("n_slots", [P, 1], I32)
        from_partner = sb("from_partner", [P, 1])
        quota = sb("quota", [P, 1])
        left = sb("left", [P, SLOTS])
        n_less_1 = sb("n_less_1", [P, 1], I32)
        last_index = sb("last_index", [P, 1], I32)
        last_slots = sb("last_slots", [P, 1])
        in_use = sb("in_use", [P, SLOTS])
        no_keys = sb("no_keys", [P, SLOTS])
        kept = sb("kept", [P, SLOTS])
        taken = sb("taken", [P, SLOTS])
        last_dots = sb("last_dots", [P, SLOTS])
        for_partner = sb("for_partner", [P, 1])
        pair_less_own = sb("pair_less_own", [P, P])
        goes_to = sb("goes_to", [P, P])
        end_j = sb("end_j", [P, J])
        end_sum = sb("end_sum", [P, J])
        top = sb("top", [P, RING + 1, SLOTS])
        size = sb("size", [P, RING + 1, SLOTS])
        code = sb("code", [P, RING + 1, SLOTS], I32)
        tab_row = sb("tab_row", [P, RING + 1, SLOTS], I32)
        tab = sb("tab", [P, RING + 1, SLOTS], I32)
        j_code = sb("j_code", [P, RING + 1, SLOTS], I32)
        side = sb("side", [P, RING + 1, SLOTS])
        j_side = sb("j_side", [P, RING + 1, SLOTS])
        j_of = sb("j_of", [P, RING + 1, SLOTS])
        flat = sb("flat", [P, RING + 1, SLOTS], U32)
        got = sb("got", [P, RING + 1, SLOTS, D])
        is_tab = sb("is_tab", [P, RING + 1, SLOTS, TPAD])
        is_j = sb("is_j", [P, RING + 1, 2 * J, SLOTS])
        is_tab_t = sb("is_tab_t", [P, 3, HALVES, P])
        products = sb("products", [P, SLOTS, D])
        dots = sb("dots", [P, SLOTS])
        by_j = sb("by_j", [P, 2 * J, SLOTS])
        round_sum = sb("round_sum", [P, 2 * J])
        acc = sb("acc", [P, 2 * J])
        wsum = sb("wsum", [P, TP])
        w_copy = sb("w_copy", [P, TP, NTOP])
        wdsum = sb("wdsum", [D, 1])
        w_cols = sb("w_cols", [D, QUADS, TPAD])
        w_diag = sb("w_diag", [P, QUADS, D])
        w_dense = sb("w_dense", [D, 1])
        bsum = sb("bsum", [D, 1])
        prods = sb("prods", [D, T + DC])
        coef = sb("coef", [P, T + DC])
        last_part = sb("last_part", [P, J, T])
        dense_part = sb("dense_part", [P, J, NF])
        last_sum = sb("last_sum", [P, J])
        dense_sum = sb("dense_sum", [P, J])
        warm = sb("warm", [1, 1])
        prob = sb("prob", [P, J])

        ps_turn = psum("ps_turn", [P, 2, 512])
        ps_wsel = psum("ps_wsel", [P, 2, SLOTS, D])
        ps_pair = psum("ps_pair", [P, 4, P])
        ps_partner = psum("ps_partner", [P, SLOTS, D])
        ps_w = psum("ps_w", [P, 3, P])
        ps_coef = psum("ps_coef", [P, 2, 256])

        first_idx_in = sem("first_idx_in")
        rest_idx_in = sem("rest_idx_in")
        weights_in = sem("weights_in")
        small_in = sem("small_in")
        iotas_ready = sem("iotas_ready")
        vec = sem("vec")
        vec_pick = sem("vec_pick")
        vec_sum = sem("vec_sum")
        consts_ready = sem("consts_ready")
        diag_ready = sem("diag_ready")
        spread = sem("spread")
        pair_ready = sem("pair_ready")
        partner_rows = sem("partner_rows")
        slots_ready = sem("slots_ready")
        wsum_ready = sem("wsum_ready")
        w_moved = sem("w_moved")
        w_cols_ready = sem("w_cols_ready")
        w_in_rows = sem("w_in_rows")
        w_ready = sem("w_ready")
        rows_turned = sem("rows_turned")
        prods_ready = sem("prods_ready")
        coef_ready = sem("coef_ready")
        flat_ready = sem("flat_ready")
        gathered = [sem(f"gathered{b}") for b in range(RING)]
        masks_ready = sem("masks_ready")
        turned = sem("turned")
        copied = sem("copied")
        selected = sem("selected")
        used = sem("used")
        logit_ready = sem("logit_ready")
        prob_ready = sem("prob_ready")
        stored = sem("stored")
        vec_last = sem("vec_last")
        last_flat_ready = sem("last_flat_ready")
        last_masks_ready = sem("last_masks_ready")
        last_turned = sem("last_turned")
        last_copied = sem("last_copied")
        last_selected = sem("last_selected")
        last_gathered = [sem(f"last_gathered{s}") for s in range(SLOTS)]
        vec_tail = sem("vec_tail")
        end_ready = sem("end_ready")

        their_rows = ps_partner[:, :, :].rearrange("p s d -> p (s d)")[:, 0:L]

        block = ctx.enter_context(nc.Block())

        NSUM = 4
        NPICK_OWN = 8
        NPICK = 12

        def ring_turns(eng, full, one_round):
            rounds_left = eng.alloc_register("rounds_left")
            eng.reg_alu(rounds_left, full - RING, MIN_FULL - RING, op=ALU.max)
            more = eng.snap(rounds_left, min_val=MIN_FULL - RING, max_val=MAX_ROUNDS - 1 - RING)
            for span in SPANS:
                made = eng.snap(more // (RING * 2 * span) * (2 * span), min_val=0, max_val=sum(SPANS))
                with eng.If(made * RING + span * RING <= more):
                    with eng.Fori(0, span) as one:
                        turn = eng.snap(made + one + 1, min_val=1, max_val=sum(SPANS))
                        for h in range(RING):
                            one_round(turn, h, True)
            whole = eng.snap(more // RING, min_val=0, max_val=sum(SPANS))

            def rest(h):
                with eng.If(whole * RING + h < more):
                    one_round(eng.snap(whole + 1, min_val=1, max_val=sum(SPANS) + 1), h, False)
                    if h + 2 < RING:
                        rest(h + 1)

            rest(0)

        def load_slots(eng):
            eng.wait_ge(slots_ready, 1)
            n = eng.value_load(n_slots[0:1, 0:1], min_val=MIN_FULL * SLOTS + 1, max_val=L)
            full_rounds = eng.alloc_register("full_rounds")
            eng.reg_alu(full_rounds, (n - 1) // SLOTS, MIN_FULL, op=ALU.max)
            full = eng.snap(full_rounds, min_val=MIN_FULL, max_val=MAX_ROUNDS - 1)
            return full, eng.snap(n - full * SLOTS, min_val=1, max_val=SLOTS)

        def later_last_slots(eng, in_last, one_slot, s=1):
            with eng.If(in_last > s):
                one_slot(s)
                if s + 1 < SLOTS:
                    later_last_slots(eng, in_last, one_slot, s + 1)

        @block.sync
        def _(sp):
            indices = sparse.rearrange("(p j) t -> p j t", p=P)
            sp.dma_start(idx[:, REST:J, :], indices[:, REST:J, :]).then_inc(first_idx_in, 16)
            sp.dma_start(idx[:, 0:REST, :], indices[:, 0:REST, :]).then_inc(rest_idx_in, 16)
            sp.dma_start(wt_sb[:, :, :], w_top[0:T * D, :].rearrange("(c q) n -> q c n", q=P)).then_inc(weights_in, 16)
            sp.dma_start(wd_sb[:, :], w_top[T * D:T * D + D, :]).then_inc(weights_in, 16)
            sp.wait_ge(prob_ready, 1)
            sp.dma_start(out.rearrange("(p j) -> p j", p=P), prob[:, :]).then_inc(stored, 16)
            sp.wait_ge(stored, 16)

        @block.gpsimd
        def _(pool):
            def iota(tile, pattern, base=0, per_partition=0):
                pool.iota(tile, pattern, base=base, channel_multiplier=per_partition,
                          allow_small_or_imprecise_dtypes=True).then_inc(iotas_ready, 1)

            iota(iota_t[:, :], [[1, TPAD]])
            iota(iota_j[:, 0, :], [[1, J]], base=1)
            iota(iota_j[:, 1, :], [[-1, J]], base=-1)
            iota(iota_col[:, :], [[1, P]])
            iota(iota_row[:, :], [[0, 1]], per_partition=1)
            iota(iota_slot[:, :], [[-1, SLOTS]], base=-OWN)

            due = pool.alloc_register("due")
            pool.reg_mov(due, 1)

            def gather(b, s):
                pool.indirect_dma_start(
                    got[:, b, s, :], None, table_rows,
                    bass.IndirectOffsetOnAxis(ap=flat[:, b, s:s + 1], axis=0),
                ).then_inc(gathered[b], 16)

            for b in range(RING):
                pool.wait_ge(flat_ready, b + 1)
                for s in range(SLOTS):
                    gather(b, s)
            full, in_last = load_slots(pool)
            pool.reg_mov(due, RING + 1)

            def gather_round(turn, b, followed):
                pool.wait_ge(flat_ready, due)
                pool.reg_add(due, due, 1)
                for s in range(SLOTS):
                    gather(b, s)

            ring_turns(pool, full, gather_round)

            def gather_last(s):
                pool.indirect_dma_start(
                    got[:, LAST_ROUND, s, :], None, table_rows,
                    bass.IndirectOffsetOnAxis(ap=flat[:, LAST_ROUND, s:s + 1], axis=0),
                ).then_inc(last_gathered[s], 16)

            were_due = pool.alloc_register("were_due")
            were_full = pool.alloc_register("were_full")
            pool.reg_alu(were_due, due, 1, op=ALU.subtract)
            pool.reg_alu(were_full, were_due, MIN_FULL, op=ALU.max)
            pool.wait_ge(flat_ready, were_full)
            pool.wait_ge(last_flat_ready, 1)
            later_last_slots(pool, in_last, gather_last)
            gather_last(0)

        @block.scalar
        def _(act):
            act.dma_start(dense_sb[:, :, :], dense.rearrange("(p j) f -> p j f", p=P)).then_inc(small_in, 16)
            act.dma_start(last_rows[:, :], tables[:, LAST, :]).then_inc(small_in, 16)
            act.dma_start(wbot_sb[:, 0:NF], w_bot_t).then_inc(small_in, 16)
            act.dma_start(wbot_sb[:, NF:DC], b_bot.rearrange("(d o) -> d o", o=1)).then_inc(small_in, 16)
            act.dma_start(btop_sb[:, :], b_top.rearrange("(d n) -> d n", d=D)).then_inc(small_in, 16)
            act.wait_ge(consts_ready, 1)
            act.activation(warm[:, :], warm[:, :], ACT.Sigmoid)
            act.wait_ge(weights_in, 32)
            for c in range(TP):
                act.activation(w_copy[:, c, :], wt_sb[:, c, :], ACT.Copy, accum_out=wsum[:, c:c + 1]).then_inc(wsum_ready, 1)

            def copy_turned(r, q):
                act.wait_ge(turned, r + 1)
                act.activation(is_tab_t[:, q, :, :], ps_turn[:, q, 0:HALVES * P].rearrange("p (k c) -> p k c", k=HALVES),
                               ACT.Copy).then_inc(copied, 1)

            for r in range(RING):
                if r >= 2:
                    act.wait_ge(selected, r - 1)
                copy_turned(r, r % 2)
            full, _ = load_slots(act)

            def copy_round(turn, h, followed):
                act.wait_ge(selected, turn * RING + (h - 1))
                copy_turned(turn * RING + h, h % 2)

            ring_turns(act, full, copy_round)
            act.wait_ge(last_turned, 1)
            act.activation(is_tab_t[:, 2, :, :], ps_coef[:, 1, :].rearrange("p (k c) -> p k c", k=HALVES),
                           ACT.Copy).then_inc(last_copied, 1)
            act.wait_ge(logit_ready, 1)
            act.activation(prob[:, :], ps_pair[:, 3, 0:J], ACT.Sigmoid).then_inc(prob_ready, 1)

        @block.tensor
        def _(pe):
            def spread_diag(k):
                pe.wait_ge(diag_ready, k + 1)
                pe.matmul(ps_pair[:, k, :], ones[:, :], diag[:, k, :], start=True, stop=True).then_inc(spread, 1)

            pe.wait_ge(consts_ready, 1)
            spread_diag(0)
            spread_diag(1)
            pe.wait_ge(pair_ready, 1)
            pe.matmul(their_rows, pair[:, :], row[:, :, :], start=True, stop=True).then_inc(partner_rows, 1)
            spread_diag(2)
            pe.wait_ge(small_in, 16 * 5)
            pe.transpose(ps_w[0:D, 2, 0:T], last_rows[:, :], ident[0:T, 0:T]).then_inc(rows_turned, 1)
            pe.wait_ge(wsum_ready, TP)
            pe.matmul(ps_w[0:D, 0, 0:TP], ident[:, 0:D], wsum[:, :], start=True, stop=True)
            pe.matmul(ps_w[0:D, 0, TP:2 * TP], ident[:, D:2 * D], wsum[:, :], start=True, stop=True).then_inc(w_moved, 1)
            pe.wait_ge(w_cols_ready, 2)
            pe.matmul(ps_w[:, 1, 0:D], w_cols[:, :, :], ident[0:D, 0:D], start=True, stop=True).then_inc(w_in_rows, 1)
            pe.wait_ge(prods_ready, 1)
            pe.matmul(ps_coef[:, 0, 0:T + DC], ones[0:D, :], prods[:, :], start=True, stop=True).then_inc(coef_ready, 1)

            def turn_mask(r, b, q):
                pe.wait_ge(masks_ready, r + 1)
                for k in range(HALVES):
                    mm = pe.transpose(ps_turn[:, q, k * P:(k + 1) * P], is_tab[:, b, k * QUADS:(k + 1) * QUADS, :],
                                      ident[:, :])
                mm.then_inc(turned, 1)

            def select(r, q):
                pe.wait_ge(copied, r + 1)
                for k in range(HALVES):
                    mm = pe.matmul(ps_wsel[:, q, k * QUADS:(k + 1) * QUADS, :], is_tab_t[:, q, k, :], w_diag[:, :, :],
                                   start=True, stop=True)
                mm.then_inc(selected, 1)

            pe.wait_ge(w_ready, QUADS)
            for r in range(RING):
                turn_mask(r, r, r % 2)
                if r >= 2:
                    pe.wait_ge(used, r - 1)
                select(r, r % 2)
            full, in_last = load_slots(pe)

            def select_round(turn, h, followed):
                turn_mask(turn * RING + h, h, h % 2)
                pe.wait_ge(used, turn * RING + (h - 1))
                select(turn * RING + h, h % 2)

            ring_turns(pe, full, select_round)
            pe.wait_ge(last_masks_ready, 1)
            for k in range(HALVES):
                mm = pe.transpose(ps_coef[:, 1, k * P:(k + 1) * P], is_tab[:, LAST_ROUND, k * QUADS:(k + 1) * QUADS, :],
                                  ident[:, :])
            mm.then_inc(last_turned, 1)
            pe.wait_ge(last_copied, 1)
            for k in range(HALVES):
                mm = pe.matmul(ps_partner[:, k * QUADS:(k + 1) * QUADS, :], is_tab_t[:, 2, k, :], w_diag[:, :, :],
                               start=True, stop=True)
            mm.then_inc(last_selected, 1)
            tail_steps = pe.alloc_register("tail_steps")
            pe.wait_ge(vec_sum, full * NSUM)
            pe.reg_alu(tail_steps, in_last * 2 - 1, 1, op=ALU.max)
            pe.wait_ge(vec_tail, tail_steps)
            pe.matmul(ps_pair[:, 3, 0:J], ident[:, :], acc[:, 0:J], start=True, stop=False)
            pe.matmul(ps_pair[:, 3, 0:J], pair[:, :], acc[:, J:2 * J], start=False, stop=False)
            pe.wait_ge(end_ready, 2)
            pe.matmul(ps_pair[:, 3, 0:J], goes_to[:, :], end_sum[:, :], start=False, stop=True).then_inc(logit_ready, 1)

        @block.vector
        def _(v):
            v.memset(ones[:, :], 1.0).then_inc(vec, 1)
            v.memset(w_diag[:, :, :], 0.0).then_inc(vec, 1)
            v.memset(w_cols[:, :, :], 0.0).then_inc(vec, 1)
            v.memset(acc[:, :], 0.0).then_inc(vec, 1)
            v.memset(warm[:, :], 1.0).then_inc(vec, 1)
            v.wait_ge(iotas_ready, 3)
            v.tensor_scalar(j_part[:, :], iota_j[:, 0, :], float(1 << J_SHIFT), None, ALU.mult).then_inc(vec, 1)
            v.wait_ge(vec, 6)
            v.scalar_tensor_tensor(out=key_base[:, :, :], in0=iota_t[:, None, 0:T].broadcast_to([P, J, T]),
                                   scalar=float(1 << ROW_BITS), in1=j_part[:, :, None].broadcast_to([P, J, T]),
                                   op0=ALU.mult, op1=ALU.add).then_inc(vec, 1)
            v.wait_ge(iotas_ready, 5)
            v.tensor_scalar(ident[:, :], iota_col[:, :], iota_row[:, :], None, ALU.is_equal).then_inc(consts_ready, 1)

            def read_keys(before, j0, j1, nth):
                js = slice(j0, j1)
                v.tensor_scalar(wrap[:, js, :], idx[:, js, :], 0.0, float(VOCAB), ALU.is_lt, ALU.mult).then_inc(vec, 1)
                v.wait_ge(vec, before + 1)
                v.scalar_tensor_tensor(out=row[:, js, :], in0=idx[:, js, :], scalar=float(LAST), in1=wrap[:, js, :],
                                       op0=ALU.min, op1=ALU.add).then_inc(vec, 1)
                v.wait_ge(vec, before + 2)
                v.tensor_scalar(at_last[:, js, :], row[:, js, :], float(LAST), 0.0, ALU.is_ge, ALU.add,
                                accum_out=n_last[:, nth:nth + 1]).then_inc(vec, 1)
                v.scalar_tensor_tensor(out=key_all[:, js, :], in0=row[:, js, :], scalar=0.0, in1=key_base[:, js, :],
                                       op0=ALU.max, op1=ALU.add).then_inc(vec, 1)
                v.wait_ge(vec, before + 4)
                v.scalar_tensor_tensor(out=keys[:, 0, js, :], in0=at_last[:, js, :], scalar=-NOTHING, in1=key_all[:, js, :],
                                       op0=ALU.mult, op1=ALU.add).then_inc(vec, 1)

            def pick(before, b, candidates, partners):
                is_last = b == LAST_ROUND
                vec_pick, flat_ready, masks_ready = pick_sems[is_last]
                v.max(top[:, b, :], candidates).then_inc(vec_pick, 1)
                v.wait_ge(vec_pick, before + 1)
                if partners:
                    v.scalar_tensor_tensor(out=size[:, b, :], in0=top[:, b, :], scalar=-1.0, in1=top[:, b, :],
                                           op0=ALU.mult, op1=ALU.max).then_inc(vec_pick, 1)
                    before += 1
                    v.wait_ge(vec_pick, before + 1)
                    v.tensor_scalar(code[:, b, :], size[:, b, :], IDLE, None, ALU.min).then_inc(vec_pick, 1)
                else:
                    v.tensor_scalar(code[:, b, :], top[:, b, :], 0.0, None, ALU.max).then_inc(vec_pick, 1)
                v.wait_ge(vec_pick, before + 2)
                v.tensor_scalar(tab[:, b, :], code[:, b, :], ROW_BITS, (1 << TAB_BITS) - 1, ALU.logical_shift_right,
                                ALU.bitwise_and).then_inc(vec_pick, 1)
                v.tensor_scalar(tab_row[:, b, :], code[:, b, :], (1 << J_SHIFT) - 1, None,
                                ALU.bitwise_and).then_inc(vec_pick, 1)
                v.wait_ge(vec_pick, before + 4)
                v.scalar_tensor_tensor(out=flat[:, b, :], in0=tab[:, b, :], scalar=float(VOCAB - (1 << ROW_BITS)),
                                       in1=tab_row[:, b, :], op0=ALU.mult, op1=ALU.add).then_inc(flat_ready, 1)
                v.tensor_tensor(is_tab[:, b, :, :], tab[:, b, :, None].broadcast_to([P, SLOTS, TPAD]),
                                iota_t[:, None, :].broadcast_to([P, SLOTS, TPAD]), ALU.is_equal).then_inc(masks_ready, 1)
                if is_last:
                    v.tensor_tensor(kept[:, :], top[:, b, :], in_use[:, :], ALU.mult).then_inc(vec, 1)
                    v.wait_ge(vec, 58)
                    v.tensor_tensor(taken[:, :], kept[:, :], no_keys[:, :], ALU.add).then_inc(vec, 1)
                    v.wait_ge(vec, 59)
                    v.match_replace(keys_row[:, :], taken[:, :], keys_row[:, :], -NOTHING).then_inc(vec_pick, 1)
                else:
                    v.match_replace(candidates, top[:, b, :], candidates, -NOTHING).then_inc(vec_pick, 1)
                v.tensor_scalar(j_code[:, b, :], code[:, b, :], J_SHIFT, None,
                                ALU.logical_shift_right).then_inc(vec_pick, 1)
                if partners:
                    v.tensor_scalar(side[:, b, :], top[:, b, :], 0.0, -2.0, ALU.is_lt, ALU.mult).then_inc(vec_pick, 1)
                    v.wait_ge(vec_pick, before + 7)
                    v.scalar_tensor_tensor(out=j_side[:, b, :], in0=side[:, b, :], scalar=1.0, in1=j_code[:, b, :],
                                           op0=ALU.add, op1=ALU.mult).then_inc(vec_pick, 1)
                    v.wait_ge(vec_pick, before + 8)
                    v.scalar_tensor_tensor(out=j_of[:, b, :], in0=left[:, :], scalar=0.0, in1=j_side[:, b, :],
                                           op0=ALU.is_gt, op1=ALU.mult).then_inc(vec_pick, 1)
                    v.tensor_scalar(left[:, :], left[:, :], last_slots[:, :] if is_last else float(SLOTS), None,
                                    ALU.subtract).then_inc(vec_pick, 1)
                    v.wait_ge(vec_pick, before + 9)
                else:
                    v.wait_ge(vec_pick, before + 6)
                    v.tensor_copy(j_of[:, b, :], j_code[:, b, :]).then_inc(vec_pick, 1)
                    v.wait_ge(vec_pick, before + 7)
                v.tensor_tensor(is_j[:, b, :, :], j_of[:, b, None, :].broadcast_to([P, 2 * J, SLOTS]),
                                iota_j[:, :, :].rearrange("p o j -> p (o j)")[:, :, None].broadcast_to([P, 2 * J, SLOTS]),
                                ALU.is_equal).then_inc(vec_pick, 1)

            pick_sems = {False: (vec_pick, flat_ready, masks_ready), True: (vec_last, last_flat_ready, last_masks_ready)}

            def add_up(r, picks, landed, b, q):
                before = r * NSUM
                v.wait_ge(vec_pick, picks)
                v.wait_ge(selected, r + 1)
                v.wait_ge(gathered[b], landed)
                v.tensor_tensor(products[:, :, :], got[:, b, :, :], ps_wsel[:, q, :, :], ALU.mult).then_inc(used, 1)
                v.wait_ge(used, r + 1)
                v.tensor_reduce(dots[:, :], products[:, :, :], AX.X, ALU.add).then_inc(vec_sum, 1)
                v.wait_ge(vec_sum, before + 1)
                v.tensor_tensor(by_j[:, :, :], is_j[:, b, :, :], dots[:, None, :].broadcast_to([P, 2 * J, SLOTS]),
                                ALU.mult).then_inc(vec_sum, 1)
                v.wait_ge(vec_sum, before + 2)
                v.tensor_reduce(round_sum[:, :], by_j[:, :, :], AX.X, ALU.add).then_inc(vec_sum, 1)
                v.wait_ge(vec_sum, before + 3)
                v.tensor_tensor(acc[:, :], acc[:, :], round_sum[:, :], ALU.add).then_inc(vec_sum, 1)

            own_keys = keys[:, 0, :, :].rearrange("p j t -> p (j t)")
            all_keys = keys[:, :, :, :].rearrange("p o j t -> p (o j t)")

            v.wait_ge(vec, 7)
            v.wait_ge(first_idx_in, 16)
            read_keys(7, REST, J, 0)
            v.wait_ge(vec, 12)
            pick(0, 0, keys[:, 0, REST:J, :].rearrange("p j t -> p (j t)"), False)
            v.wait_ge(rest_idx_in, 16)
            read_keys(12, 0, REST, 1)
            v.wait_ge(vec, 17)

            v.tensor_scalar(missed[:, :], n_last[:, 0:1], -float(FIRST * T - SLOTS), 0.0, ALU.add, ALU.max).then_inc(vec, 1)
            v.tensor_tensor(n_last_all[:, :], n_last[:, 0:1], n_last[:, 1:2], ALU.add).then_inc(vec, 1)
            v.wait_ge(vec, 19)
            v.tensor_tensor(n_minus[:, :], missed[:, :], n_last_all[:, :], ALU.subtract).then_inc(vec, 1)
            v.wait_ge(vec, 20)
            v.tensor_scalar(n_own[:, :], n_minus[:, :], float(L), None, ALU.add).then_inc(vec, 1)
            v.wait_ge(vec, 21)
            v.tensor_scalar(mix[:, :], n_own[:, :], float(P), iota_row[:, :], ALU.mult, ALU.add).then_inc(vec, 1)
            v.wait_ge(vec, 22)
            v.wait_ge(consts_ready, 1)
            v.tensor_scalar(diag[:, 0, :], ident[:, :], mix[:, :], None, ALU.mult).then_inc(diag_ready, 1)
            pick(NPICK_OWN, 1, own_keys, False)
            v.wait_ge(spread, 1)
            v.tensor_scalar(greater[:, :], ps_pair[:, 0, :], mix[:, :], 0.0, ALU.is_gt, ALU.add,
                            accum_out=rank[:, :]).then_inc(vec, 1)
            v.wait_ge(vec, 23)
            v.tensor_scalar(diag[:, 1, :], ident[:, :], rank[:, :], None, ALU.mult).then_inc(diag_ready, 1)
            pick(2 * NPICK_OWN, 2, own_keys, False)
            v.wait_ge(spread, 2)
            v.tensor_scalar(pair[:, :], ps_pair[:, 1, :], rank[:, :], float(P - 1), ALU.add,
                            ALU.is_equal).then_inc(pair_ready, 1)
            v.wait_ge(pair_ready, 1)
            v.tensor_tensor(pair_mix[:, :], pair[:, :], ps_pair[:, 0, :], ALU.mult).then_inc(vec, 1)
            v.wait_ge(vec, 24)
            v.tensor_reduce(mix_partner[:, :], pair_mix[:, :], AX.X, ALU.add).then_inc(vec, 1)
            v.wait_ge(vec, 25)
            v.tensor_copy(mix_int[:, :], mix_partner[:, :]).then_inc(vec, 1)
            v.wait_ge(vec, 26)
            v.tensor_scalar(n_partner[:, :], mix_int[:, :], P.bit_length() - 1, None,
                            ALU.logical_shift_right).then_inc(vec, 1)
            v.tensor_scalar(own_slots[:, :], n_own[:, :], float(OWN), None, ALU.max).then_inc(vec, 1)
            v.wait_ge(vec, 28)
            v.tensor_scalar(own_1[:, :], own_slots[:, :], 1.0, None, ALU.add).then_inc(vec, 1)
            v.tensor_copy(n_partner_f[:, :], n_partner[:, :]).then_inc(vec, 1)
            v.wait_ge(vec, 30)
            v.scalar_tensor_tensor(out=pair_sum[:, :], in0=n_partner_f[:, :], scalar=float(OWN), in1=own_1[:, :],
                                   op0=ALU.max, op1=ALU.add).then_inc(vec, 1)
            v.wait_ge(vec, 31)
            v.tensor_scalar(pair_mean[:, :], pair_sum[:, :], 1, None, ALU.logical_shift_right).then_inc(vec, 1)
            v.wait_ge(vec, 32)
            v.tensor_scalar(pair_mean_f[:, :], pair_mean[:, :], float(MIN_FULL * SLOTS + 1), None, ALU.max).then_inc(vec, 1)
            v.wait_ge(vec, 33)
            v.tensor_scalar(diag[:, 2, :], ident[:, :], pair_mean_f[:, :], None, ALU.mult).then_inc(diag_ready, 1)
            pick(3 * NPICK_OWN, 3, own_keys, False)
            v.wait_ge(spread, 3)
            v.tensor_reduce(n_slots_f[:, :], ps_pair[:, 2, :], AX.X, ALU.max).then_inc(vec, 1)
            v.wait_ge(vec, 34)
            v.tensor_copy(n_slots[:, :], n_slots_f[:, :]).then_inc(slots_ready, 1)
            v.tensor_scalar(from_partner[:, :], n_partner_f[:, :], n_slots_f[:, :], 0.0,
                            ALU.subtract, ALU.max).then_inc(vec, 1)
            v.wait_ge(vec, 35)
            v.tensor_scalar(quota[:, :], from_partner[:, :], own_slots[:, :], n_slots_f[:, :],
                            ALU.add, ALU.min).then_inc(vec, 1)
            v.wait_ge(vec, 36)
            v.wait_ge(iotas_ready, 6)
            v.tensor_scalar(left[:, :], iota_slot[:, :], quota[:, :], None, ALU.add).then_inc(vec, 1)

            v.wait_ge(weights_in, 32)
            v.tensor_reduce(wdsum[:, :], wd_sb[:, :], AX.X, ALU.add).then_inc(vec, 1)
            v.wait_ge(small_in, 16 * 5)
            v.tensor_reduce(bsum[:, :], btop_sb[:, :], AX.X, ALU.add).then_inc(vec, 1)
            v.wait_ge(vec, 38)
            v.tensor_scalar(w_dense[:, :], wdsum[:, :], 1.0 / NTOP, None, ALU.mult).then_inc(vec, 1)
            v.wait_ge(w_moved, 1)
            for o in range(2):
                v.tensor_scalar(w_cols[:, :, o:T:2], ps_w[0:D, 0, None, o * TP:(o + 1) * TP].broadcast_to([D, QUADS, TP]),
                                1.0 / NTOP, None, ALU.mult).then_inc(w_cols_ready, 1)
            v.wait_ge(vec, 40)
            v.tensor_scalar(prods[:, T:T + DC], wbot_sb[:, :], w_dense[:, :], None, ALU.mult).then_inc(vec, 1)
            v.wait_ge(w_in_rows, 1)
            for k in range(QUADS):
                own = slice(k * TPAD, (k + 1) * TPAD)
                v.tensor_copy(w_diag[own, k, :], ps_w[own, 1, 0:D]).then_inc(w_ready, 1)
            v.wait_ge(rows_turned, 1)
            v.tensor_tensor(prods[:, 0:T], w_cols[:, 0, 0:T], ps_w[0:D, 2, 0:T], ALU.mult).then_inc(vec, 1)
            v.wait_ge(vec, 42)
            v.scalar_tensor_tensor(out=prods[:, T + NF:T + DC], in0=bsum[:, :], scalar=1.0 / NTOP,
                                   in1=prods[:, T + NF:T + DC], op0=ALU.mult, op1=ALU.add).then_inc(prods_ready, 1)

            v.wait_ge(partner_rows, 1)
            row_of = their_rows.rearrange("p (j t) -> p j t", j=J)
            v.scalar_tensor_tensor(out=key_all[:, :, :], in0=row_of, scalar=0.0, in1=key_base[:, :, :],
                                   op0=ALU.max, op1=ALU.add).then_inc(vec, 1)
            v.tensor_scalar(partner_last[:, :, :], row_of, float(LAST), None, ALU.is_ge).then_inc(vec, 1)
            v.wait_ge(vec, 44)
            v.scalar_tensor_tensor(out=keys[:, 1, :, :], in0=partner_last[:, :, :], scalar=-NOTHING, in1=key_all[:, :, :],
                                   op0=ALU.mult, op1=ALU.subtract).then_inc(vec, 1)

            v.wait_ge(coef_ready, 1)
            v.tensor_copy(coef[:, :], ps_coef[:, 0, 0:T + DC]).then_inc(vec, 1)
            v.wait_ge(vec, 46)
            v.tensor_tensor(last_part[:, :, :], at_last[:, :, :], coef[:, None, 0:T].broadcast_to([P, J, T]),
                            ALU.mult).then_inc(vec, 1)
            v.tensor_tensor(dense_part[:, :, :], dense_sb[:, :, :], coef[:, None, T:T + NF].broadcast_to([P, J, NF]),
                            ALU.mult).then_inc(vec, 1)
            v.wait_ge(vec, 48)
            v.tensor_reduce(last_sum[:, :], last_part[:, :, :], AX.X, ALU.add).then_inc(vec, 1)
            v.tensor_reduce(dense_sum[:, :], dense_part[:, :, :], AX.X, ALU.add).then_inc(vec, 1)
            v.wait_ge(vec, 50)
            v.scalar_tensor_tensor(out=acc[:, 0:J], in0=dense_sum[:, :], scalar=coef[:, T + NF:T + DC], in1=last_sum[:, :],
                                   op0=ALU.add, op1=ALU.add).then_inc(vec, 1)
            v.wait_ge(vec, 51)

            for r in range(RING):
                add_up(r, (r + 1) * NPICK_OWN, SLOTS * 16, r, r % 2)
                pick(RING * NPICK_OWN + r * NPICK, r, all_keys, True)

            v.memset(keys_row[:, 2 * L:2 * L + SLOTS], -NO_KEY).then_inc(vec, 1)
            v.tensor_scalar(n_less_1[:, :], n_slots_f[:, :], -1.0, None, ALU.add).then_inc(vec, 1)
            v.wait_ge(vec, 53)
            v.tensor_scalar(last_index[:, :], n_less_1[:, :], SLOTS - 1, None, ALU.bitwise_and).then_inc(vec, 1)
            v.wait_ge(vec, 54)
            v.tensor_scalar(last_slots[:, :], last_index[:, :], 1.0, None, ALU.add).then_inc(vec, 1)
            v.wait_ge(vec, 55)
            v.tensor_scalar(in_use[:, :], iota_slot[:, :], last_slots[:, :], -float(OWN), ALU.add, ALU.is_gt).then_inc(vec, 1)
            v.wait_ge(vec, 56)
            v.tensor_scalar(no_keys[:, :], in_use[:, :], -1.0, NO_KEY, ALU.add, ALU.mult).then_inc(vec, 1)
            pick(0, LAST_ROUND, all_keys, True)

            v.wait_ge(vec_last, NPICK)
            v.tensor_scalar(for_partner[:, :], side[:, LAST_ROUND, 0:1], -0.5, None, ALU.mult).then_inc(vec, 1)
            v.tensor_tensor(pair_less_own[:, :], pair[:, :], ident[:, :], ALU.subtract).then_inc(vec, 1)
            v.wait_ge(vec, 61)
            v.scalar_tensor_tensor(out=goes_to[:, :], in0=pair_less_own[:, :], scalar=for_partner[:, :], in1=ident[:, :],
                                   op0=ALU.mult, op1=ALU.add).then_inc(vec_tail, 1)
            v.tensor_tensor(end_j[:, :], is_j[:, LAST_ROUND, 0:J, 0], is_j[:, LAST_ROUND, J:2 * J, 0],
                            ALU.add).then_inc(vec, 1)

            full, in_last = load_slots(v)

            def sum_round(turn, h, followed):
                r = turn * RING + h
                picked_before = RING * NPICK_OWN + (r - RING) * NPICK
                add_up(r, picked_before + NPICK, turn * (SLOTS * 16) + SLOTS * 16, h, h % 2)
                if followed:
                    with v.If(r + RING < full):
                        pick(picked_before + RING * NPICK, h, all_keys, True)

            ring_turns(v, full, sum_round)

            def dot_last(s):
                v.wait_ge(last_gathered[s], 16)
                return v.scalar_tensor_tensor(out=products[:, s, :], in0=got[:, LAST_ROUND, s, :], scalar=1.0,
                                              in1=ps_partner[:, s, :], op0=ALU.mult, op1=ALU.mult,
                                              accum_out=last_dots[:, s:s + 1])

            def sum_last(s):
                dot_last(s).then_inc(vec_tail, 1)
                v.wait_ge(vec_tail, 2 * s)
                v.scalar_tensor_tensor(out=acc[:, :], in0=is_j[:, LAST_ROUND, :, s], scalar=last_dots[:, s:s + 1],
                                       in1=acc[:, :], op0=ALU.mult, op1=ALU.add).then_inc(vec_tail, 1)

            v.wait_ge(last_selected, 1)
            v.wait_ge(vec_sum, full * NSUM)
            v.wait_ge(vec, 62)
            later_last_slots(v, in_last, sum_last)
            dot_last(0).then_inc(end_ready, 1)
            v.wait_ge(end_ready, 1)
            v.tensor_scalar(end_sum[:, :], end_j[:, :], last_dots[:, 0:1], None, ALU.mult).then_inc(end_ready, 1)


def kernel(**inputs):
    import numpy as _np
    import concourse.bacc as _bacc
    from concourse import mybir as _mybir
    from concourse.bass_utils import run_bass_kernel_spmd as _run

    nc = _bacc.Bacc("TRN2", target_bir_lowering=False, num_devices=1)
    given = {
        "dense": inputs["r_dense_features"],
        "sparse": inputs["r_sparse_features"],
        "tables": inputs["L0_rec_tables"],
        "w_bot_t": _np.ascontiguousarray(_np.asarray(inputs["L0_rec_W_bot"]).T),
        "b_bot": inputs["L0_rec_b_bot"],
        "w_top": inputs["L0_rec_W_top"],
        "b_top": inputs["L0_rec_b_top"],
    }
    arrays, args = {}, []
    for name, a in given.items():
        a = _np.ascontiguousarray(a)
        arrays[f"in_{name}"] = a
        args.append(nc.dram_tensor(f"in_{name}", a.shape, _mybir.dt.from_np(a.dtype), kind="ExternalInput").ap())
    batch = arrays["in_dense"].shape[0]
    args.append(nc.dram_tensor("out_prob", (batch,), _mybir.dt.float32, kind="ExternalOutput").ap())
    recommender_head(nc, *args)
    r = _run(nc, [arrays], core_ids=[0])
    return r.results[0]["out_prob"]
```
